# Optimizing a Trainium2 kernel written in Bass

```python
import numpy as np
import jax
import jax.numpy as jnp

def _softmax(x, axis=-1):
    return jax.nn.softmax(x, axis=axis)

def _gelu(x):
    return jax.nn.gelu(x, approximate=True)

def _silu(x):
    return jax.nn.silu(x)

def _sigmoid(x):
    return jax.nn.sigmoid(x)

def _layernorm(x, axis=-1, eps=1e-05):
    m = jnp.mean(x, axis=axis, keepdims=True)
    v = jnp.var(x, axis=axis, keepdims=True)
    return (x - m) / jnp.sqrt(v + eps)

def _scatter_add(tgt, idx, src, axis=0):
    return tgt.at[idx].add(src)

def _segment_sum(src, seg, n):
    return jax.ops.segment_sum(src, seg, n)
kernel_name = 'mk_metaformer_d1_conv_nchw128_r2_260359'

def setup_inputs(seed: int=0):
    np.random.seed(seed)
    _w = jnp.asarray

    def _rec_inputs():
        import jax
        import jax.numpy as jnp
        _gk = jax.random.key(seed)
        x = -0.0001636 + 1 * jax.random.normal(jax.random.fold_in(_gk, 1), (16, 64, 112, 112), jnp.float32)
        return x
    x = _rec_inputs()

    def _L0_conv_setup():
        import jax, jax.numpy as jnp
        import numpy as np
        key = jax.random.key(seed)
        k1, k2, k3 = jax.random.split(key, 3)
        B, C, H, W = (16, 64, 112, 112)
        x = jax.random.normal(k1, (B, C, H, W), dtype=jnp.float32)
        fan_in = 2 * 3 * 3
        bound = 1.0 / np.sqrt(fan_in)
        conv_w = jax.random.uniform(k2, (1, 2, 3, 3), jnp.float32, -bound, bound)
        conv_b = jax.random.uniform(k3, (1,), jnp.float32, -bound, bound)
        return {'x': x, 'conv_w': conv_w, 'conv_b': conv_b}
    _L0_conv_all = _L0_conv_setup()
    _L0_conv_in = {k: v for k, v in _L0_conv_all.items() if k in ('conv_w', 'conv_b')}
    del _L0_conv_all

    def _L0_ffn_setup():
        import jax, jax.numpy as jnp
        import numpy as np
        B, N, D, C, E, K = (8, 4096, 64, 64, 8, 2)
        key = jax.random.key(seed)
        k0, k1, k2 = jax.random.split(key, 3)
        x = jax.random.normal(k0, (B, N, D), dtype=jnp.float32)
        router_w = jax.random.normal(k1, (D, E), dtype=jnp.float32) * 0.05
        router_b = jnp.zeros((E,), dtype=jnp.float32)
        expert_w = jax.random.normal(k2, (E, D, C), dtype=jnp.float32) * (1.0 / np.sqrt(D))
        expert_b = jnp.zeros((E, C), dtype=jnp.float32)
        return {'x': x, 'router_w': router_w, 'router_b': router_b, 'expert_w': expert_w, 'expert_b': expert_b}
    _L0_ffn_all = _L0_ffn_setup()
    _L0_ffn_in = {k: v for k, v in _L0_ffn_all.items() if k in ('router_w', 'router_b', 'expert_w', 'expert_b')}
    del _L0_ffn_all
    return {'x': x, 'L0_conv_conv_w': _L0_conv_in['conv_w'], 'L0_conv_conv_b': _L0_conv_in['conv_b'], 'L0_ffn_router_w': _L0_ffn_in['router_w'], 'L0_ffn_router_b': _L0_ffn_in['router_b'], 'L0_ffn_expert_w': _L0_ffn_in['expert_w'], 'L0_ffn_expert_b': _L0_ffn_in['expert_b']}

def reference(x, L0_conv_conv_w, L0_conv_conv_b, L0_ffn_router_w, L0_ffn_router_b, L0_ffn_expert_w, L0_ffn_expert_b):
    import jax
    import jax.numpy as jnp

    def _L0_conv_ref(x, conv_w, conv_b):
        import jax, jax.numpy as jnp
        import numpy as np
        pooled = jnp.stack([jnp.max(x, axis=1), jnp.mean(x, axis=1)], axis=1)
        y = jax.lax.conv_general_dilated(pooled, conv_w, window_strides=(1, 1), padding=((1, 1), (1, 1)), dimension_numbers=('NCHW', 'OIHW', 'NCHW')) + conv_b[None, :, None, None]
        scale = jax.nn.sigmoid(y)
        return x * scale

    def _L0_ffn_ref(x, router_w, router_b, expert_w, expert_b):
        import jax, jax.numpy as jnp
        import numpy as np
        B, N, D, C, E, K = (8, 4096, 64, 64, 8, 2)
        router_probs = jax.nn.softmax(x @ router_w + router_b, axis=-1)
        top_p, top_i = jax.lax.top_k(router_probs, K)
        top_p = top_p / jnp.sum(top_p, axis=-1, keepdims=True)
        expert_out = jnp.einsum('bnd,edc->bnec', x, expert_w) + expert_b
        gathered = jnp.take_along_axis(expert_out, top_i[..., None], axis=2)
        return jnp.einsum('bnk,bnkc->bnc', top_p, gathered)

    def _gn(v, G=32, eps=1e-05):
        B_, C_, H_, W_ = v.shape
        g = v.reshape(B_, G, C_ // G, H_, W_)
        m = jnp.mean(g, axis=(2, 3, 4), keepdims=True)
        s = jnp.var(g, axis=(2, 3, 4), keepdims=True)
        return ((g - m) / jnp.sqrt(s + eps)).reshape(v.shape)

    def _ln_c(v, eps=1e-06):
        m = jnp.mean(v, axis=1, keepdims=True)
        s = jnp.var(v, axis=1, keepdims=True)
        return (v - m) / jnp.sqrt(s + eps)

    def _ln_t(v, eps=1e-05):
        m = jnp.mean(v, axis=-1, keepdims=True)
        s = jnp.var(v, axis=-1, keepdims=True)
        return (v - m) / jnp.sqrt(s + eps)

    def _to_tokens(v):
        B_, C_, H_, W_ = v.shape
        return v.reshape(B_, C_, H_ * W_).transpose(0, 2, 1)

    def _from_tokens(t, like):
        B_, C_, H_, W_ = like.shape
        return t.transpose(0, 2, 1).reshape(B_, C_, H_, W_)
    x = x + _L0_conv_ref(_ln_c(x), L0_conv_conv_w, L0_conv_conv_b)
    t = _to_tokens(x)
    t = t + _L0_ffn_ref(_ln_t(t), L0_ffn_router_w, L0_ffn_router_b, L0_ffn_expert_w, L0_ffn_expert_b)
    x = _from_tokens(t, x)
    return x

_drawn_inputs = setup_inputs


def setup_inputs(seed=0):
    import zlib

    import numpy as np

    out = dict(_drawn_inputs(seed))
    spreads = {'L0_ffn_router_b': (0.0, 0.1), 'L0_ffn_expert_b': (0.0, 0.1)}
    factors = {}
    for name, (base, spread) in spreads.items():
        noise = np.random.default_rng([zlib.crc32(name.encode()), seed]).standard_normal(out[name].shape)
        drawn = base * np.exp(spread * noise) if base else spread * noise
        out[name] = jnp.asarray(drawn.astype(out[name].dtype))
    for name, factor in factors.items():
        out[name] = (out[name] * factor).astype(out[name].dtype)
    return out
```

```python
from contextlib import ExitStack

import numpy as np

import concourse.bass as bass
from concourse import mybir

F32 = mybir.dt.float32
BF16 = mybir.dt.bfloat16
F16 = mybir.dt.float16
ALU = mybir.AluOpType
ACT = mybir.ActivationFunctionType
AX = mybir.AxisListType

B, CH, H, W = 16, 64, 112, 112
E = 8
P = 128
PAIRS = B // 2
ROWS = 8
STEPS = H // ROWS
TOK = ROWS * W
HALF = TOK // 2
GRP = 2
NGRP = ROWS // GRP
KT = E // 2
UNITS = 2 * KT
T1N = P + 2 * E + 2
LN = 2 * E + 2
QN_ = 2 * E + 2
SR = 3 * 2 * QN_
QG, QB, QA, QM = 0, E, 2 * E, 2 * E + 1
EPS1, EPS2 = 1e-6, 1e-5
BIG = 1e30
ROUNDS = PAIRS + 2


def constant_arrays():
    f = np.zeros((P, 2 * P + 2 + 3 * W + E), np.float32)
    for b in range(2):
        lo = b * CH
        f[lo:lo + CH, lo:lo + CH] = np.eye(CH) - 1.0 / CH
        f[lo:lo + CH, P + b] = 1.0 / CH
    o = P + 2
    for kw in range(3):
        for w_out in range(W):
            w_in = w_out + kw - 1
            if 0 <= w_in < W:
                f[w_in, o + kw * W + w_out] = 1.0
    o += 3 * W
    f[:, o:o + E] = np.arange(E, 0, -1)
    o += E
    for part in range(3):
        for b in range(2):
            f[part * 2 * QN_ + b * QN_ + QM, o + b * CH:o + (b + 1) * CH] = -1.0
    g = np.zeros((P, (UNITS + 1) * P + P), np.float32)
    for part in range(3):
        for b in range(2):
            row = part * 2 * QN_ + b * QN_
            for k in range(KT):
                for e in range(2):
                    lo = (2 * k + b) * P + e * CH
                    g[row + QG + 2 * k + e, lo:lo + CH] = 1.0
            g[row + QA, UNITS * P + b * CH:UNITS * P + (b + 1) * CH] = 1.0
    g[:, (UNITS + 1) * P:] = np.eye(P)
    return f, g


def gated_expert_program(nc, x, conv_w, conv_b, router_w, router_b, expert_w, expert_b, const_f, const_g, out):
    xv = x.rearrange("(q b) c h w -> q (b c) (h w)", b=2)
    ov = out.rearrange("(q b) c h w -> q (b c) (h w)", b=2)

    with ExitStack() as ctx:
        def sb(name, shape, dt=F32):
            return ctx.enter_context(nc.sbuf_tensor(name, shape, dt))

        def ps(name, shape, dt=F32):
            return ctx.enter_context(nc.psum_tensor(name, shape, dt))

        def sem(name):
            return ctx.enter_context(nc.semaphore(name))

        cf = sb("cf", [P, 2 * P + 2 + 3 * W + E])
        cg = sb("cg", [P, (UNITS + 2) * P], BF16)
        gx = sb("gx", [P, 4, TOK])
        gx_flat = gx[:, :, :].rearrange("p a t -> p (a t)")
        centre = cf[:, 0:P]
        mean_cols = cf[:, P:P + 2]
        shift = [cf[0:W, P + 2 + kw * W:P + 2 + (kw + 1) * W] for kw in range(3)]
        prio_c = P + 2 + 3 * W
        prio = cf[0:W, prio_c:prio_c + E]
        bias_c = prio_c + E
        bias_base = cf[0:SR, bias_c:bias_c + P]
        cg_load = gx_flat[:, 0:(UNITS + 2) * P]
        ident = cg[0:W, (UNITS + 1) * P:(UNITS + 1) * P + W]
        rhs1 = sb("rhs1", [P, T1N])
        wr = sb("wr", [P, 2 * E])
        wst = sb("wst", [P, KT * CH])
        wc = sb("wc", [P, KT * CH])
        bh = sb("bh", [SR, P], F16)
        bl = sb("bl", [SR, P], F16)
        cwb = sb("cwb", [W, 18])
        ncb = sb("ncb", [W, 1])
        brb = sb("brb", [W, E])
        band = sb("band", [W, 6, W])
        eps = sb("eps", [W, 2])
        low = sb("low", [W, 1])
        xa = sb("xa", [P, 2, TOK])
        xsq = sb("xsq", [W, 2, 2, 2 * ROWS, CH])
        tree = sb("tree", [W, 32 * 62])
        la = sb("la", [W, H, LN])
        st = sb("st", [W, 3, 2 * H])
        lb = sb("lb", [W, H, LN])
        stb = sb("stb", [W, 3, 2 * H])
        pooled = sb("pooled", [W, 2, 2, H + 2])
        std = sb("std", [W, 2 * H])
        r1 = sb("r1", [W, 2 * H])
        ex = sb("ex", [W, 2 * H])
        sg = sb("sg", [W, 2 * H])
        av = sb("av", [W, 2 * H])
        v2 = sb("v2", [W, 2 * H])
        rho = sb("rho", [W, 2 * H])
        top1 = sb("top1", [W, 2 * H])
        key_max = sb("key_max", [W, 2 * H])
        top2 = sb("top2", [W, 2 * H])
        g1 = sb("g1", [W, 2 * H])
        g2 = sb("g2", [W, 2 * H])
        lg = sb("lg", [W, 2 * H, E])
        dl = sb("dl", [W, 2 * H, E])
        key = sb("key", [W, 2 * H, E], BF16)
        oh1 = sb("oh1", [W, 2 * H, E], BF16)
        ge = sb("ge", [W, 2 * H, E], BF16)
        oh2 = sb("oh2", [W, 2 * H, E], BF16)
        qn = sb("qn", [W, 2 * H, QN_])
        q = sb("q", [W, H, 2 * QN_])
        res = sb("res", [W, 2, ROWS, 2 * QN_])
        parts = sb("parts", [W, 2, ROWS, 3, 2 * QN_], BF16)
        s = sb("s", [SR, 2, TOK], BF16)
        xd = sb("xd", [P, 2, 2, TOK])
        xc = sb("xc", [P, 2, TOK])
        a1s = sb("a1s", [P, TOK])
        tt = sb("tt", [P, 2, TOK])
        ot = sb("ot", [P, 2, TOK])

        gb = ps("gb", [P, 4, 512])
        moe = ps("moe", [P, 2, 512])
        t1 = ps("t1", [P, 512])
        misc = ps("misc", [P, 512])
        misc16 = misc[:, :].bitcast(BF16)

        ld_const = sem("ld_const")
        ld_bias = sem("ld_bias")
        setup_pe = sem("setup_pe")
        setup_dve = sem("setup_dve")
        setup_pool = sem("setup_pool")
        setup_step = sem("setup_step")
        ld_xa = [sem(f"ld_xa{i}") for i in range(2)]
        ld_xd = [[sem(f"ld_xd{i}{b}") for b in range(2)] for i in range(2)]
        ld_xc = [sem(f"ld_xc{i}") for i in range(2)]
        stored = [sem(f"stored{i}") for i in range(2)]
        centred = sem("centred")
        centred_out = sem("centred_out")
        squared = sem("squared")
        maxed = sem("maxed")
        summed = sem("summed")
        snap = sem("snap")
        b_act = sem("b_act")
        b_dve = sem("b_dve")
        b_pool = sem("b_pool")
        convolved = sem("convolved")
        q_ready = sem("q_ready")
        part1 = sem("part1")
        rest1 = sem("rest1")
        part2 = sem("part2")
        part3 = sem("part3")
        turned = sem("turned")
        s_ready = sem("s_ready")
        spread = sem("spread")
        scaled = sem("scaled")
        a1_spread = sem("a1_spread")
        a1_out = sem("a1_out")
        scaled_x = sem("scaled_x")
        mixed = sem("mixed")
        final = sem("final")

        LOADS = 8 * 16

        def at(r, first, per, n):
            return (r - first) * per + n if isinstance(r, int) else r * per + (n - first * per)

        def due(count):
            return not isinstance(count, int) or count > 0

        def a_at(r, per_step, step, n):
            return at(r, 0, per_step * STEPS, per_step * step + n)

        def b_at(r, per_round, n):
            return at(r, 1, per_round, n)

        def c_at(r, per_step, step, n):
            return at(r, 2, per_step * STEPS, per_step * step + n)

        def slot_at(r, first, step, add):
            return at(r, first, add * STEPS // 2, add * (step // 2 + 1))

        B_DVE, B_POOL, B_ACT, SNAPS, LEVELS = 23, 10, 3, 3, 6

        def run_rounds(body):
            body(0, True, False, False)
            body(1, True, True, False)
            body(2, True, True, True)
            return (3, PAIRS), ((PAIRS, False, True, True), (PAIRS + 1, False, False, True))

        def first_pair(r):
            return isinstance(r, int) and r == 2

        def follows(step, n, Bp, C):
            return C if step + n < STEPS else Bp

        by_image = "w (h b) -> w b h"

        def wide(v):
            return v[:, :].unsqueeze(2).to_broadcast([W, 2 * H, E])

        prios = prio.unsqueeze(1).to_broadcast([W, 2 * H, E])

        block = ctx.enter_context(nc.Block())

        @block.sync
        def _(sp):
            for dst, src in (
                (cf[:, :], const_f),
                (cg_load, const_g),
                (wst[:, :].rearrange("p (k c) -> p k c", k=KT), expert_w.rearrange("(k e) d c -> (e d) k c", e=2)),
                (cwb[:, :], conv_w.rearrange("o c h w -> o (c h w)").to_broadcast([W, 18])),
                (ncb[:, :], conv_b.rearrange("(o n) -> o n", o=1).to_broadcast([W, 1])),
                (brb[:, :], router_b.rearrange("(o n) -> o n", o=1).to_broadcast([W, E])),
            ):
                sp.dma_start(dst, src).then_inc(ld_const, 16)
            sp.wait_ge(setup_dve, 1)
            sp.dma_start(wr[0:CH, 0:E], router_w).then_inc(ld_const, 16)
            sp.dma_start(wr[CH:P, E:2 * E], router_w).then_inc(ld_const, 16)
            sp.wait_ge(ld_const, LOADS)
            for part in range(3):
                for b in range(2):
                    row = part * 2 * QN_ + b * QN_ + QB
                    col = bias_c + b * CH
                    sp.dma_start(cf[row:row + E, col:col + CH], expert_b).then_inc(ld_bias, 16)

            def load_a(r, pairs, step):
                if due(count := a_at(r, NGRP, step - 1, 0)):
                    sp.wait_ge(centred, count)
                src = xv[bass.ds(pairs[0], 1), :, step * TOK:(step + 1) * TOK].rearrange("a p t -> p (a t)")
                sp.dma_start(xa[:, step % 2, :], src).then_inc(ld_xa[step % 2], 16)

            def load_c(pairs, step):
                sl = step % 2
                pair = pairs[2] if step < STEPS else pairs[1]
                cols = slice((step % STEPS) * TOK, (step % STEPS + 1) * TOK)
                for b in range(2):
                    src = xv[bass.ds(pair, 1), b * CH:(b + 1) * CH, cols].rearrange("a p t -> p (a t)")
                    for half in range(2):
                        sp.dma_start(xd[half * CH:(half + 1) * CH, sl, b, :], src).then_inc(ld_xd[sl][b], 16)
                src = xv[bass.ds(pair, 1), :, cols].rearrange("a p t -> p (a t)")
                sp.dma_start(xc[:, sl, :], src).then_inc(ld_xc[sl], 16)

            def store(pairs, step):
                pair = pairs[2] if step >= 0 else pairs[3]
                n = step % STEPS
                dst = ov[bass.ds(pair, 1), :, n * TOK:(n + 1) * TOK].rearrange("a p t -> p (a t)")
                sp.dma_start(dst, ot[:, step % 2, :]).then_inc(stored[step % 2], 16)

            def body(r, A, Bp, C):
                pairs = [r - n if isinstance(r, int) else sp.snap(r - n) for n in range(4)]
                if A:
                    load_a(r, pairs, 0)
                for step in range(STEPS):
                    if A and step < STEPS - 1:
                        load_a(r, pairs, step + 1)
                    stores = C and not (first_pair(r) and step == 0)
                    if stores:
                        if due(count := c_at(r, 2, step - 1, 2)):
                            sp.wait_ge(final, count)
                    if follows(step, 1, Bp, C):
                        load_c(pairs, step + 1)
                    if stores:
                        store(pairs, step - 1)

            loop, rest = run_rounds(body)
            with sp.Fori(*loop) as r:
                body(r, True, True, True)
            for args in rest:
                body(*args)
            if due(count := c_at(PAIRS + 1, 2, STEPS - 1, 2)):
                sp.wait_ge(final, count)
            store([None, None, PAIRS - 1], STEPS - 1)
            for sl in range(2):
                sp.wait_ge(stored[sl], 16 * PAIRS * STEPS // 2)

        @block.tensor
        def _(pe):
            pe.wait_ge(ld_const, LOADS)
            pe.matmul(gb[:, 0, 0:KT * CH], centre, wst[:, :], start=True, stop=True)
            pe.matmul(gb[:, 1, 0:2 * E], centre, wr[:, :], start=True, stop=True).then_inc(setup_pe, 1)
            pe.wait_ge(setup_dve, 2)
            pe.wait_ge(setup_pool, 2)

            def centre_rows(r, step, g):
                if g == 0:
                    if due(count := slot_at(r, 0, step, 16)):
                        pe.wait_ge(ld_xa[step % 2], count)
                if due(count := a_at(r, NGRP, step, g)):
                    pe.wait_ge(centred_out, count)
                for j in range(GRP):
                    row = g * GRP + j
                    last = pe.matmul(t1[0:W, j * T1N:(j + 1) * T1N], xa[:, step % 2, row * W:(row + 1) * W],
                                     rhs1[:, :], start=True, stop=True)
                last.then_inc(centred, 1)

            def turn(r, step, Bp, C):
                if due(count := c_at(r, 1, step, 1)):
                    pe.wait_ge(part3, count)
                if due(count := c_at(r, 2, step - 2, 2)):
                    pe.wait_ge(a1_out, count)
                if Bp and (step == 4 or not C):
                    if due(count := b_at(r, B_ACT, 1)):
                        pe.wait_ge(b_act, count)
                for j in range(ROWS):
                    last = pe.transpose(misc16[0:SR, j * W:(j + 1) * W],
                                        parts[:, step % 2, j, :, :].rearrange("w a c -> w (a c)"), ident)
                last.then_inc(turned, 1)

            def spread_unit(r, step, u):
                if u >= UNITS:
                    step, u = step + 1, u - UNITS
                if u == 0:
                    if due(count := c_at(r, 1, step, 1)):
                        pe.wait_ge(s_ready, count)
                if due(count := c_at(r, UNITS, step, u - 1)):
                    pe.wait_ge(scaled, count)
                for c in range(2):
                    last = pe.matmul(gb[:, 2 * (u % 2) + c, 0:HALF], cg[0:SR, u * P:(u + 1) * P],
                                     s[:, step % 2, c * HALF:(c + 1) * HALF], start=True, stop=True)
                last.then_inc(spread, 1)

            def spread_a1(r, step, c, turned_next):
                if c == 0 and turned_next:
                    if due(count := c_at(r, 1, step + 1, 1)):
                        pe.wait_ge(s_ready, count)
                else:
                    if due(count := c_at(r, 2, step, c)):
                        pe.wait_ge(a1_out, count)
                pe.matmul(misc[:, 0:HALF], cg[0:SR, UNITS * P:(UNITS + 1) * P],
                          s[:, step % 2, c * HALF:(c + 1) * HALF], start=True, stop=True).then_inc(a1_spread, 1)

            def biases(r, step):
                for c in range(2):
                    if due(count := c_at(r, 2, step - 1, c + 1)):
                        pe.wait_ge(final, count)
                    for n, w in enumerate((bh, bl)):
                        pe.matmul(moe[:, c, 0:HALF], w[:, :], s[:, step % 2, c * HALF:(c + 1) * HALF],
                                  start=(n == 0), stop=False, skip_group_check=True)

            def experts(r, step, k, c):
                if c == 0:
                    if due(count := c_at(r, UNITS, step, 2 * k + 2)):
                        pe.wait_ge(scaled, count)
                for b in range(2):
                    last = pe.matmul(moe[b * CH:(b + 1) * CH, c, 0:HALF], wc[:, k * CH:(k + 1) * CH],
                                     gx[:, (2 * k + b) % 4, c * HALF:(c + 1) * HALF],
                                     start=False, stop=(k == KT - 1), skip_group_check=True)
                last.then_inc(mixed, 1)

            def convolve(r, C):
                if due(count := b_at(r, B_DVE, 3)):
                    pe.wait_ge(b_dve, count)
                if C:
                    if due(count := c_at(r, 2, 2, 2)):
                        pe.wait_ge(a1_out, count)
                for n in range(6):
                    ch, kh = n // 3, n % 3
                    last = pe.matmul(misc[0:W, 0:2 * H].rearrange("w (b h) -> w b h", b=2), band[:, n, :],
                                     pooled[:, ch, :, kh:kh + H], start=(n == 0), stop=(n == 5))
                last.then_inc(convolved, 1)

            def body(r, A, Bp, C):
                if first_pair(r):
                    spread_unit(r, 0, 2)
                    spread_unit(r, 0, 3)
                for step in range(STEPS):
                    ahead = follows(step, 1, Bp, C)
                    if ahead:
                        turn(r, step + 1, Bp, C)
                    for k in range(KT):
                        if A and k == 0:
                            centre_rows(r, step, 0)
                        if C:
                            if k == 0:
                                biases(r, step)
                            experts(r, step, k, 0)
                        if A and k > 0:
                            centre_rows(r, step, k)
                        if C:
                            if k < KT - 2 or ahead:
                                spread_unit(r, step, 2 * k + 4)
                            experts(r, step, k, 1)
                            if k in (1, 2):
                                spread_a1(r, step, k - 1, ahead)
                        if Bp and step == 2 and k == KT - 1:
                            convolve(r, C)
                        if C and (k < KT - 2 or ahead):
                            spread_unit(r, step, 2 * k + 5)
                if Bp and not C:
                    spread_unit(r, STEPS, 0)
                    spread_unit(r, STEPS, 1)

            loop, rest = run_rounds(body)
            with pe.Fori(*loop) as r:
                body(r, True, True, True)
            for args in rest:
                body(*args)

        @block.vector
        def _(dve):
            dve.memset(wr[:, :], 0.0).then_inc(setup_dve, 1)
            dve.memset(eps[:, 0:1], EPS1)
            dve.memset(eps[:, 1:2], EPS2)
            dve.wait_ge(ld_const, LOADS)
            done = [0]

            def link(ins):
                done[0] += 1
                ins.then_inc(setup_step, 1)
                dve.wait_ge(setup_step, done[0])

            for n in range(6):
                link(dve.tensor_scalar(band[:, n, :], shift[0], cwb[:, 3 * n:3 * n + 1], None, ALU.mult))
                for kw in (1, 2):
                    link(dve.scalar_tensor_tensor(out=band[:, n, :], in0=shift[kw],
                                                  scalar=cwb[:, 3 * n + kw:3 * n + kw + 1], in1=band[:, n, :],
                                                  op0=ALU.mult, op1=ALU.add))
            link(dve.tensor_copy(cg[:, :], cg_load))
            link(dve.tensor_copy(rhs1[:, 0:P], centre))
            link(dve.tensor_copy(rhs1[:, P + 2 * E:T1N], mean_cols))
            dve.wait_ge(setup_pe, 1)
            link(dve.tensor_copy(wc[:, :], gb[:, 0, 0:KT * CH]))
            link(dve.tensor_copy(rhs1[:, P:P + 2 * E], gb[:, 1, 0:2 * E]))
            dve.wait_ge(ld_bias, 6 * 16)
            link(dve.tensor_copy(bh[:, :], bias_base))
            link(dve.tensor_tensor(bl[:, :], bias_base, bh[:, :], ALU.subtract))
            dve.tensor_scalar(ncb[:, :], ncb[:, :], -1.0, None, ALU.mult).then_inc(setup_dve, 1)

            def channel_max(r, step):
                if due(count := a_at(r, NGRP, step, NGRP)):
                    dve.wait_ge(centred_out, count)
                n = step % STEPS
                dve.tensor_reduce(st[:, 0, 2 * ROWS * n:2 * ROWS * (n + 1)], xsq[:, step % 2, 0, :, :],
                                  AX.X, ALU.max).then_inc(maxed, 1)

            def scale_unit(r, step, u):
                sl, b = step % 2, u % 2
                if u < 2:
                    if due(count := slot_at(r, 2, step, 32)):
                        dve.wait_ge(ld_xd[sl][b], count)
                if due(count := c_at(r, UNITS, step, u + 1)):
                    dve.wait_ge(spread, count)
                if due(count := c_at(r, 2 * KT, step, 2 * (u // 2) - 2)):
                    dve.wait_ge(mixed, count)
                dve.tensor_tensor(gx[:, u % 4, :].rearrange("p (c t) -> p c t", c=2),
                                  gb[:, 2 * (u % 2):2 * (u % 2) + 2, 0:HALF],
                                  xd[:, sl, b, :].rearrange("p (c t) -> p c t", c=2), ALU.mult).then_inc(scaled, 1)

            def finish(r, step, c):
                sl = step % 2
                if c == 0:
                    if due(count := c_at(r, 1, step, 1)):
                        dve.wait_ge(scaled_x, count)
                    if due(count := slot_at(r, 2, step - 2, 16)):
                        dve.wait_ge(stored[sl], count)
                if due(count := c_at(r, 2 * KT, step, 2 * KT - 1 + c)):
                    dve.wait_ge(mixed, count)
                cols = slice(c * HALF, (c + 1) * HALF)
                dve.tensor_tensor(ot[:, sl, cols], moe[:, c, 0:HALF], tt[:, sl, cols], ALU.add).then_inc(final, 1)

            def gate(r, step):
                def own(n):
                    if due(count := b_at(r, B_DVE, n)):
                        dve.wait_ge(b_dve, count)

                if step == 1:
                    if due(count := b_at(r, SNAPS, 3)):
                        dve.wait_ge(snap, count)
                    if due(count := b_at(r, 1, 0)):
                        dve.wait_ge(convolved, count)
                    dve.reciprocal(r1[:, :], std[:, :]).then_inc(b_dve, 1)
                    own(1)
                    dve.tensor_tensor(pooled[:, 0, :, 1:H + 1], stb[:, 0, :].rearrange(by_image, b=2),
                                      r1[:, :].rearrange(by_image, b=2), ALU.mult).then_inc(b_dve, 1)
                    dve.scalar_tensor_tensor(out=pooled[:, 1, :, 1:H + 1], in0=stb[:, 1, :].rearrange(by_image, b=2),
                                             scalar=1.0 / CH, in1=r1[:, :].rearrange(by_image, b=2),
                                             op0=ALU.mult, op1=ALU.mult).then_inc(b_dve, 1)
                elif step == 3:
                    if due(count := b_at(r, B_ACT, 1)):
                        dve.wait_ge(b_act, count)
                    if due(count := b_at(r, 1, 0)):
                        dve.wait_ge(q_ready, count)
                    dve.tensor_scalar(sg[:, :], ex[:, :], 1.0, None, ALU.add).then_inc(b_dve, 1)
                    own(4)
                    dve.reciprocal(v2[:, :], sg[:, :]).then_inc(b_dve, 1)
                    own(5)
                    dve.tensor_tensor(av[:, :], v2[:, :], r1[:, :], ALU.mult).then_inc(b_dve, 1)
                    own(6)
                    dve.tensor_scalar(qn[:, :, QA], av[:, :], 1.0, None, ALU.add).then_inc(b_dve, 1)
                    dve.tensor_tensor(qn[:, :, QM].rearrange("w (h b) -> w h b", b=2),
                                      av[:, :].rearrange("w (h b) -> w h b", b=2), lb[:, :, 2 * E:LN],
                                      ALU.mult).then_inc(b_dve, 1)
                    own(7)
                    dve.tensor_tensor(sg[:, :], qn[:, :, QA], qn[:, :, QA], ALU.mult).then_inc(b_dve, 1)
                    own(9)
                    dve.tensor_tensor(v2[:, :], sg[:, :], stb[:, 2, :], ALU.mult).then_inc(b_dve, 1)
                elif step == 4:
                    if due(count := b_at(r, B_ACT, 2)):
                        dve.wait_ge(b_act, count)
                    dve.reciprocal(sg[:, :], std[:, :]).then_inc(b_dve, 1)
                    own(11)
                    dve.tensor_tensor(rho[:, :], sg[:, :], qn[:, :, QA], ALU.mult).then_inc(b_dve, 1)
                elif step == 5:
                    if due(count := b_at(r, B_POOL, 2)):
                        dve.wait_ge(b_pool, count)
                    dve.tensor_reduce(top1[:, :], lg[:, :, :], AX.X, ALU.max).then_inc(b_dve, 1)
                elif step == 6:
                    if due(count := b_at(r, B_POOL, 3)):
                        dve.wait_ge(b_pool, count)
                    dve.scalar_tensor_tensor(out=key[:, :, :], in0=dl[:, :, :], scalar=0.0, in1=prios,
                                             op0=ALU.is_ge, op1=ALU.mult).then_inc(b_dve, 1)
                    own(14)
                    dve.tensor_reduce(key_max[:, :], key[:, :, :], AX.X, ALU.max).then_inc(b_dve, 1)
                elif step == 7:
                    own(15)
                    dve.tensor_tensor(oh1[:, :, :], prios, wide(key_max), ALU.is_equal).then_inc(b_dve, 1)
                elif step == 8:
                    if due(count := b_at(r, B_POOL, 5)):
                        dve.wait_ge(b_pool, count)
                    dve.tensor_reduce(top2[:, :], lg[:, :, :], AX.X, ALU.max).then_inc(b_dve, 1)
                    own(17)
                    dve.tensor_tensor(ge[:, :, :], lg[:, :, :], wide(top2), ALU.is_ge).then_inc(b_dve, 1)
                elif step == 9:
                    if due(count := b_at(r, B_POOL, 6)):
                        dve.wait_ge(b_pool, count)
                    dve.tensor_reduce(key_max[:, :], key[:, :, :], AX.X, ALU.max).then_inc(b_dve, 1)
                    own(19)
                    dve.tensor_tensor(oh2[:, :, :], prios, wide(key_max), ALU.is_equal).then_inc(b_dve, 1)
                    if due(count := b_at(r, B_ACT, 3)):
                        dve.wait_ge(b_act, count)
                    dve.tensor_scalar(sg[:, :], ex[:, :], 1.0, None, ALU.add).then_inc(b_dve, 1)
                    own(21)
                    dve.reciprocal(g1[:, :], sg[:, :]).then_inc(b_dve, 1)
                    own(22)
                    dve.tensor_tensor(g2[:, :], ex[:, :], g1[:, :], ALU.mult).then_inc(b_dve, 1)

            def reduce_and_gate(r, step, A, Bp):
                if Bp:
                    gate(r, step)
                    if step == 0:
                        channel_max(r, -1)
                if A and step > 0:
                    if step == 1:
                        if due(count := b_at(r, SNAPS, 2)):
                            dve.wait_ge(snap, count)
                    channel_max(r, step - 1)

            def body(r, A, Bp, C):
                for step in range(STEPS):
                    if not C:
                        reduce_and_gate(r, step, A, Bp)
                        continue
                    for u in range(UNITS):
                        scale_unit(r, step, u)
                        if u < 2 and not (first_pair(r) and step == 0):
                            finish(r, step - 1, u)
                        if u == 3:
                            reduce_and_gate(r, step, A, Bp)

            loop, rest = run_rounds(body)
            with dve.Fori(*loop) as r:
                body(r, True, True, True)
            for args in rest:
                body(*args)
            for c in range(2):
                finish(PAIRS + 1, STEPS - 1, c)

        @block.scalar
        def _(act):
            act.wait_ge(setup_dve, 2)

            def centred_to_sbuf(r, step, g):
                sl = step % 2
                if g == 0:
                    if due(count := a_at(r, LEVELS, step - 1, 0)):
                        act.wait_ge(summed, count)
                    if due(count := a_at(r, 1, step - 1, 0)):
                        act.wait_ge(maxed, count)
                if due(count := a_at(r, NGRP, step, g + 1)):
                    act.wait_ge(centred, count)
                src = t1[0:W, 0:GRP * T1N].rearrange("w (j n) -> w j n", j=GRP)
                act.activation(xsq[:, sl, 0, 2 * GRP * g:2 * GRP * (g + 1), :]
                               .rearrange("w (j b) c -> w j (b c)", b=2), src[:, :, 0:P], ACT.Copy)
                row = step * ROWS + g * GRP
                act.activation(la[:, row:row + GRP, :], src[:, :, P:T1N], ACT.Copy).then_inc(centred_out, 1)

            def square(r, step):
                if due(count := a_at(r, NGRP, step, NGRP)):
                    act.wait_ge(centred_out, count)
                act.activation(xsq[:, step % 2, 1, :, :], xsq[:, step % 2, 0, :, :], ACT.Square) \
                   .then_inc(squared, 1)

            def part_one(r, step):
                n = step % STEPS
                if due(count := c_at(r, 1, step - 2, 1)):
                    act.wait_ge(turned, count)
                if due(count := b_at(r, 1, step // STEPS)):
                    act.wait_ge(q_ready, count)
                act.activation(parts[:, step % 2, :, 0, :], q[:, n * ROWS:(n + 1) * ROWS, :], ACT.Copy) \
                   .then_inc(part1, 1)

            def part_two(r, step):
                if due(count := c_at(r, 1, step, 1)):
                    act.wait_ge(rest1, count)
                act.activation(parts[:, step % 2, :, 1, :], res[:, step % 2, :, :], ACT.Copy).then_inc(part2, 1)

            def turned_to_sbuf(r, step):
                if due(count := c_at(r, 1, step, 1)):
                    act.wait_ge(turned, count)
                if due(count := c_at(r, 2 * KT, step - 2, 2 * KT)):
                    act.wait_ge(mixed, count)
                act.activation(s[:, step % 2, :], misc16[0:SR, 0:TOK], ACT.Copy).then_inc(s_ready, 1)

            def a1_to_sbuf(r, step, c):
                if due(count := c_at(r, 2, step, c + 1)):
                    act.wait_ge(a1_spread, count)
                if c == 0:
                    if due(count := c_at(r, 1, step - 1, 1)):
                        act.wait_ge(scaled_x, count)
                act.activation(a1s[:, c * HALF:(c + 1) * HALF], misc[:, 0:HALF], ACT.Copy).then_inc(a1_out, 1)

            def gate(r, step, A, C):
                if step == 0:
                    if due(count := a_at(r, 1, 0, 0)):
                        act.wait_ge(maxed, count)
                    if due(count := a_at(r, LEVELS, 0, 0)):
                        act.wait_ge(summed, count)
                    act.activation(stb[:, :, :], st[:, :, :], ACT.Copy).then_inc(snap, 1)
                    if due(count := b_at(r, SNAPS, 2)):
                        act.wait_ge(snap, count)
                    act.activation(std[:, :], stb[:, 2, :], ACT.Sqrt, bias=eps[:, 0:1], scale=1.0 / CH) \
                       .then_inc(snap, 1)
                elif step == 2:
                    if due(count := b_at(r, 1, 1)):
                        act.wait_ge(convolved, count)
                    act.activation(ex[:, :].rearrange(by_image, b=2), misc[0:W, 0:2 * H].rearrange("w (b h) -> w b h", b=2),
                                   ACT.Exp, bias=ncb[:, :], scale=-1.0).then_inc(b_act, 1)
                elif step == 3:
                    if due(count := b_at(r, B_DVE, 10)):
                        act.wait_ge(b_dve, count)
                    act.activation(std[:, :], v2[:, :], ACT.Sqrt, bias=eps[:, 1:2], scale=1.0 / CH).then_inc(b_act, 1)
                elif step == 8:
                    if due(count := b_at(r, B_DVE, 17)):
                        act.wait_ge(b_dve, count)
                    act.activation(ex[:, :], top2[:, :], ACT.Exp).then_inc(b_act, 1)

            def body(r, A, Bp, C):
                for step in range(STEPS):
                    if Bp and step == 0:
                        if due(count := a_at(r, NGRP, 0, 0)):
                            act.wait_ge(centred_out, count)
                        if due(count := b_at(r, B_DVE, 0)):
                            act.wait_ge(b_dve, count)
                        if due(count := b_at(r, B_POOL, 0)):
                            act.wait_ge(b_pool, count)
                        act.activation(lb[:, :, :], la[:, :, :], ACT.Copy).then_inc(snap, 1)
                        if due(count := b_at(r, SNAPS, 1)):
                            act.wait_ge(snap, count)
                    if follows(step, 1, Bp, C):
                        turned_to_sbuf(r, step + 1)
                    if A:
                        centred_to_sbuf(r, step, 0)
                    if Bp and step == STEPS - 2:
                        if due(count := b_at(r, B_POOL, B_POOL)):
                            act.wait_ge(b_pool, count)
                        if due(count := c_at(r, 1, STEPS, 0)):
                            act.wait_ge(rest1, count)
                        act.activation(q[:, :, :], qn[:, :, :].rearrange("w (h b) k -> w h (b k)", b=2), ACT.Copy) \
                           .then_inc(q_ready, 1)
                    if follows(step, 2, Bp, C):
                        part_one(r, step + 2)
                    for g in range(1, NGRP):
                        if A:
                            centred_to_sbuf(r, step, g)
                        if C and g < 3:
                            a1_to_sbuf(r, step, g - 1)
                    if follows(step, 2, Bp, C):
                        part_two(r, step + 2)
                    if Bp:
                        gate(r, step, A, C)
                    if A:
                        square(r, step)

            loop, rest = run_rounds(body)
            with act.Fori(*loop) as r:
                body(r, True, True, True)
            for args in rest:
                body(*args)

        @block.gpsimd
        def _(pool):
            pool.memset(low[:, :], -BIG).then_inc(setup_pool, 1)
            pool.memset(pooled[:, :, :, :], 0.0).then_inc(setup_pool, 1)
            pool.wait_ge(setup_pool, 2)

            def channel_sums(r, step):
                if due(count := a_at(r, 1, step, 1)):
                    pool.wait_ge(squared, count)
                src = xsq[:, step % 2, :, :, :].rearrange("w k g c -> w (k g) c")
                at_, n = 0, CH // 2
                for level in range(LEVELS):
                    if due(count := a_at(r, LEVELS, step, level)):
                        pool.wait_ge(summed, count)
                    if n > 1:
                        dst = tree[:, at_:at_ + 4 * ROWS * n].rearrange("w (g c) -> w g c", c=n)
                        pool.tensor_tensor(dst, src[:, :, 0:n], src[:, :, n:2 * n], ALU.add).then_inc(summed, 1)
                        at_ += 4 * ROWS * n
                        src = dst
                    else:
                        cols = slice(2 * ROWS * (step % STEPS), 2 * ROWS * (step % STEPS + 1))
                        kg = src.rearrange("w (k g) c -> w k g c", k=2)
                        pool.tensor_tensor(st[:, 1:3, cols], kg[:, :, :, 0], kg[:, :, :, 1], ALU.add) \
                            .then_inc(summed, 1)
                    n //= 2

            def rest_one(r, step):
                n = step % STEPS
                if due(count := c_at(r, 1, step, 1)):
                    pool.wait_ge(part1, count)
                if due(count := c_at(r, 1, step - 2, 1)):
                    pool.wait_ge(part3, count)
                pool.tensor_tensor(res[:, step % 2, :, :], q[:, n * ROWS:(n + 1) * ROWS, :],
                                   parts[:, step % 2, :, 0, :], ALU.subtract).then_inc(rest1, 1)

            def part_three(r, step):
                if due(count := c_at(r, 1, step, 1)):
                    pool.wait_ge(part2, count)
                pool.tensor_tensor(parts[:, step % 2, :, 2, :], res[:, step % 2, :, :],
                                   parts[:, step % 2, :, 1, :], ALU.subtract).then_inc(part3, 1)

            def scale_x(r, step):
                sl = step % 2
                if due(count := slot_at(r, 2, step, 16)):
                    pool.wait_ge(ld_xc[sl], count)
                if due(count := c_at(r, 2, step, 2)):
                    pool.wait_ge(a1_out, count)
                if due(count := c_at(r, 2, step - 2, 2)):
                    pool.wait_ge(final, count)
                pool.tensor_tensor(tt[:, sl, :], xc[:, sl, :], a1s[:, :], ALU.mult).then_inc(scaled_x, 1)

            def gate(r, step):
                def own(n):
                    if due(count := b_at(r, B_POOL, n)):
                        pool.wait_ge(b_pool, count)

                if step == 4:
                    if due(count := b_at(r, B_DVE, 12)):
                        pool.wait_ge(b_dve, count)
                    own(0)
                    pool.tensor_tensor(lg[:, :, :].rearrange("w (h b) e -> w h b e", b=2),
                                       lb[:, :, 0:2 * E].rearrange("w h (b e) -> w h b e", b=2),
                                       rho[:, :].rearrange("w (h b) -> w h b", b=2).unsqueeze(3)
                                       .to_broadcast([W, H, 2, E]), ALU.mult).then_inc(b_pool, 1)
                    own(1)
                    pool.tensor_tensor(lg[:, :, :], lg[:, :, :],
                                       brb[:, :].unsqueeze(1).to_broadcast([W, 2 * H, E]), ALU.add) \
                        .then_inc(b_pool, 1)
                elif step == 5:
                    if due(count := b_at(r, B_DVE, 13)):
                        pool.wait_ge(b_dve, count)
                    pool.tensor_tensor(dl[:, :, :], lg[:, :, :], wide(top1), ALU.subtract).then_inc(b_pool, 1)
                elif step == 7:
                    if due(count := b_at(r, B_DVE, 16)):
                        pool.wait_ge(b_dve, count)
                    own(3)
                    pool.tensor_tensor(lg[:, :, :], oh1[:, :, :],
                                       low[:, :].unsqueeze(2).to_broadcast([W, 2 * H, E]), ALU.mult) \
                        .then_inc(b_pool, 1)
                    own(4)
                    pool.tensor_tensor(lg[:, :, :], lg[:, :, :], dl[:, :, :], ALU.add).then_inc(b_pool, 1)
                elif step == 8:
                    if due(count := b_at(r, B_DVE, 18)):
                        pool.wait_ge(b_dve, count)
                    pool.tensor_tensor(key[:, :, :], ge[:, :, :], prios, ALU.mult).then_inc(b_pool, 1)
                elif step == 9:
                    if due(count := b_at(r, B_DVE, 23)):
                        pool.wait_ge(b_dve, count)
                    pool.tensor_tensor(lg[:, :, :], oh1[:, :, :], wide(g1), ALU.mult).then_inc(b_pool, 1)
                    pool.tensor_tensor(dl[:, :, :], oh2[:, :, :], wide(g2), ALU.mult).then_inc(b_pool, 1)
                elif step == 10:
                    own(8)
                    if due(count := b_at(r, 1, 0)):
                        pool.wait_ge(q_ready, count)
                    pool.tensor_tensor(qn[:, :, QB:QB + E], lg[:, :, :], dl[:, :, :], ALU.add).then_inc(b_pool, 1)
                    own(9)
                    pool.tensor_tensor(qn[:, :, QG:QG + E], qn[:, :, QB:QB + E], wide(rho), ALU.mult) \
                        .then_inc(b_pool, 1)

            def body(r, A, Bp, C):
                for step in range(STEPS):
                    if follows(step, 2, Bp, C):
                        rest_one(r, step + 2)
                    if Bp and step == 0:
                        channel_sums(r, -1)
                    if A and step > 0:
                        if step == 1:
                            if due(count := b_at(r, SNAPS, 2)):
                                pool.wait_ge(snap, count)
                        channel_sums(r, step - 1)
                    if follows(step, 2, Bp, C):
                        part_three(r, step + 2)
                    if C:
                        scale_x(r, step)
                    if Bp:
                        gate(r, step)

            loop, rest = run_rounds(body)
            with pool.Fori(*loop) as r:
                body(r, True, True, True)
            for args in rest:
                body(*args)


_INS = ['x', 'L0_conv_conv_w', 'L0_conv_conv_b', 'L0_ffn_router_w', 'L0_ffn_router_b', 'L0_ffn_expert_w',
        'L0_ffn_expert_b']
_OUT = ((B, CH, H, W), 'float32')


def kernel(**inputs):
    import concourse.bacc as _bacc
    from concourse.bass_utils import run_bass_kernel_spmd as _run

    nc = _bacc.Bacc("TRN2", target_bir_lowering=False, num_devices=1)
    arrays, args = {}, []
    named = [(name, np.ascontiguousarray(inputs[name])) for name in _INS]
    named += list(zip(("const_f", "const_g"), constant_arrays()))
    for name, a in named:
        arrays[f"in_{name}_dram"] = a
        args.append(nc.dram_tensor(f"in_{name}_dram", a.shape, mybir.dt.from_np(a.dtype), kind="ExternalInput").ap())
    args.append(nc.dram_tensor("out_0_dram", _OUT[0], mybir.dt.from_np(np.dtype(_OUT[1])), kind="ExternalOutput").ap())
    gated_expert_program(nc, *args)
    r = _run(nc, [arrays], core_ids=[0])
    return r.results[0]["out_0_dram"]
```

```python
from contextlib import ExitStack

import numpy as np

import concourse.bass as bass
from concourse import mybir

F32 = mybir.dt.float32
BF16 = mybir.dt.bfloat16
F16 = mybir.dt.float16
ALU = mybir.AluOpType
ACT = mybir.ActivationFunctionType
AX = mybir.AxisListType

B, CH, H, W = 16, 64, 112, 112
E = 8
P = 128
PAIRS = B // 2
ROWS = 8
STEPS = H // ROWS
TOK = ROWS * W
HALF = TOK // 2
GRP = 2
NGRP = ROWS // GRP
KT = E // 2
UNITS = 2 * KT
LN = 2 * E + 4
T1N = P + LN
EARLY = 6
QN_ = 2 * E + 2
SR = 3 * 2 * QN_
QG, QB, QA, QM = 0, E, 2 * E, 2 * E + 1
EPS1, EPS2 = 1e-6, 1e-5
BIG = 1e30
ROUNDS = PAIRS + 2


def constant_arrays():
    f = np.zeros((P, 2 * P + 2 + 3 * W + E), np.float32)
    for b in range(2):
        lo = b * CH
        f[lo:lo + CH, lo:lo + CH] = np.eye(CH) - 1.0 / CH
        f[lo:lo + CH, P + b] = 1.0 / CH
    o = P + 2
    for kw in range(3):
        for w_out in range(W):
            w_in = w_out + kw - 1
            if 0 <= w_in < W:
                f[w_in, o + kw * W + w_out] = 1.0
    o += 3 * W
    f[:, o:o + E] = np.arange(E, 0, -1)
    o += E
    for part in range(3):
        for b in range(2):
            f[part * 2 * QN_ + b * QN_ + QM, o + b * CH:o + (b + 1) * CH] = -1.0
    g = np.zeros((P, (UNITS + 1) * P + P), np.float32)
    for part in range(3):
        for b in range(2):
            row = part * 2 * QN_ + b * QN_
            for k in range(KT):
                for e in range(2):
                    lo = (2 * k + b) * P + e * CH
                    g[row + QG + 2 * k + e, lo:lo + CH] = 1.0
            g[row + QA, UNITS * P + b * CH:UNITS * P + (b + 1) * CH] = 1.0
    g[:, (UNITS + 1) * P:] = np.eye(P)
    return f, g


def gated_expert_program(nc, x, conv_w, conv_b, router_w, router_b, expert_w, expert_b, const_f, const_g, out):
    xv = x.rearrange("(q b) c h w -> q (b c) (h w)", b=2)
    ov = out.rearrange("(q b) c h w -> q (b c) (h w)", b=2)

    with ExitStack() as ctx:
        def sb(name, shape, dt=F32):
            return ctx.enter_context(nc.sbuf_tensor(name, shape, dt))

        def ps(name, shape, dt=F32):
            return ctx.enter_context(nc.psum_tensor(name, shape, dt))

        def sem(name):
            return ctx.enter_context(nc.semaphore(name))

        cf = sb("cf", [P, 2 * P + 2 + 3 * W + E])
        cg = sb("cg", [P, (UNITS + 2) * P], BF16)
        gx = sb("gx", [P, UNITS, TOK])
        gx_flat = gx[:, :, :].rearrange("p a t -> p (a t)")
        centre = cf[:, 0:P]
        mean_cols = cf[:, P:P + 2]
        shift = [cf[0:W, P + 2 + kw * W:P + 2 + (kw + 1) * W] for kw in range(3)]
        prio_c = P + 2 + 3 * W
        prio = cf[0:W, prio_c:prio_c + E]
        bias_c = prio_c + E
        bias_base = cf[0:SR, bias_c:bias_c + P]
        cg_load = gx_flat[:, 0:(UNITS + 2) * P]
        ident = cg[0:W, (UNITS + 1) * P:(UNITS + 1) * P + W]
        rhs1 = sb("rhs1", [P, T1N])
        wr = sb("wr", [P, 2 * E])
        wst = sb("wst", [P, KT * CH])
        wc = sb("wc", [P, KT * CH])
        bh = sb("bh", [SR, P], F16)
        bl = sb("bl", [SR, P], F16)
        cwb = sb("cwb", [W, 18])
        ncb = sb("ncb", [W, 1])
        brb = sb("brb", [W, E])
        band = sb("band", [W, 6, W])
        eps = sb("eps", [W, 2])
        low = sb("low", [W, 1])
        xa = sb("xa", [P, 2, TOK])
        xsq = sb("xsq", [W, 2, 2, 2 * ROWS, CH])
        tree = sb("tree", [W, 2 * ROWS * (CH - 2)])
        early_l = sb("early_l", [W, EARLY * ROWS, LN])
        early_s = sb("early_s", [W, 2, EARLY * ROWS * 2])
        logit_mean = sb("logit_mean", [W, H, LN])
        stats = sb("stats", [W, 2, 2 * H])
        pooled = sb("pooled", [W, 2, 2, H + 2])
        std = sb("std", [W, 2 * H])
        r1 = sb("r1", [W, 2 * H])
        ex = sb("ex", [W, 2 * H])
        sg = sb("sg", [W, 2 * H])
        av = sb("av", [W, 2 * H])
        ap1 = sb("ap1", [W, 2 * H])
        am = sb("am", [W, 2 * H])
        v2 = sb("v2", [W, 2 * H])
        rho = sb("rho", [W, 2 * H])
        top1 = sb("top1", [W, 2 * H])
        key_max = sb("key_max", [W, 2 * H])
        top2 = sb("top2", [W, 2 * H])
        g1 = sb("g1", [W, 2 * H])
        g2 = sb("g2", [W, 2 * H])
        lg = sb("lg", [W, 2 * H, E])
        dl = sb("dl", [W, 2 * H, E])
        key = sb("key", [W, 2 * H, E], BF16)
        oh1 = sb("oh1", [W, 2 * H, E], BF16)
        ge = sb("ge", [W, 2 * H, E], BF16)
        oh2 = sb("oh2", [W, 2 * H, E], BF16)
        q = sb("q", [W, H, 2 * QN_])
        res = sb("res", [W, 2, ROWS, 2 * QN_])
        parts = sb("parts", [W, 2, ROWS, 3, 2 * QN_], BF16)
        s = sb("s", [SR, 2, TOK], BF16)
        xd = sb("xd", [P, 2, 2, TOK])
        xc = sb("xc", [P, 2, TOK])
        a1s = sb("a1s", [P, 2, TOK])
        tt = sb("tt", [P, 2, TOK])
        ot = sb("ot", [P, 2, TOK])

        gb = ps("gb", [P, 4, 512])
        moe = ps("moe", [P, 2, 512])
        t1 = ps("t1", [P, 512])
        misc = ps("misc", [P, 512])
        misc16 = misc[:, :].bitcast(BF16)

        ld_const = sem("ld_const")
        ld_bias = sem("ld_bias")
        setup_pe = sem("setup_pe")
        setup_dve = sem("setup_dve")
        setup_pool = sem("setup_pool")
        setup_step = sem("setup_step")
        ld_xa = [sem(f"ld_xa{i}") for i in range(2)]
        ld_xd = [[sem(f"ld_xd{i}{b}") for b in range(2)] for i in range(2)]
        ld_xc = [sem(f"ld_xc{i}") for i in range(2)]
        stored = [sem(f"stored{i}") for i in range(2)]
        centred = sem("centred")
        centred_out = sem("centred_out")
        squared = sem("squared")
        maxed = sem("maxed")
        summed = sem("summed")
        joined = sem("joined")
        b_act = sem("b_act")
        b_dve = sem("b_dve")
        b_pool = sem("b_pool")
        convolved = sem("convolved")
        part1 = sem("part1")
        rest1 = sem("rest1")
        part2 = sem("part2")
        part3 = sem("part3")
        turned = sem("turned")
        s_ready = sem("s_ready")
        spread = sem("spread")
        scaled = sem("scaled")
        a1_spread = sem("a1_spread")
        a1_out = sem("a1_out")
        scaled_x = sem("scaled_x")
        mixed = sem("mixed")
        final = sem("final")

        LOADS = 8 * 16

        def at(r, first, per, n):
            return (r - first) * per + n if isinstance(r, int) else r * per + (n - first * per)

        def due(count):
            return not isinstance(count, int) or count > 0

        def a_at(r, per_step, step, n):
            return at(r, 0, per_step * STEPS, per_step * step + n)

        def b_at(r, per_round, n):
            return at(r, 1, per_round, n)

        def c_at(r, per_step, step, n):
            return at(r, 2, per_step * STEPS, per_step * step + n)

        def slot_at(r, first, step, add):
            return at(r, first, add * STEPS // 2, add * (step // 2 + 1))

        B_DVE, B_POOL, B_ACT, JOINS, LEVELS = 25, 10, 4, 2, 6

        def run_rounds(body):
            body(0, True, False, False)
            body(1, True, True, False)
            body(2, True, True, True)
            return (3, PAIRS), ((PAIRS, False, True, True), (PAIRS + 1, False, False, True))

        def first_pair(r):
            return isinstance(r, int) and r == 2

        def follows(step, n, Bp, C):
            return C if step + n < STEPS else Bp

        def centre_bank(g, C):
            return t1[:, :] if C or g % 2 == 0 else moe[:, 0, :]

        def logits_at(step):
            return (early_l, step * ROWS) if step < EARLY else (logit_mean, step * ROWS)

        def stats_at(step):
            n = step % STEPS
            return (early_s if n < EARLY else stats), slice(2 * ROWS * n, 2 * ROWS * (n + 1))

        q_tokens = q[:, :, :].rearrange("w h (b k) -> w (h b) k", b=2)
        by_image = "w (h b) -> w b h"

        def wide(v):
            return v[:, :].unsqueeze(2).to_broadcast([W, 2 * H, E])

        prios = prio.unsqueeze(1).to_broadcast([W, 2 * H, E])

        block = ctx.enter_context(nc.Block())

        @block.sync
        def _(sp):
            for dst, src in (
                (cf[:, :], const_f),
                (cg_load, const_g),
                (wst[:, :].rearrange("p (k c) -> p k c", k=KT), expert_w.rearrange("(k e) d c -> (e d) k c", e=2)),
                (cwb[:, :], conv_w.rearrange("o c h w -> o (c h w)").to_broadcast([W, 18])),
                (ncb[:, :], conv_b.rearrange("(o n) -> o n", o=1).to_broadcast([W, 1])),
                (brb[:, :], router_b.rearrange("(o n) -> o n", o=1).to_broadcast([W, E])),
            ):
                sp.dma_start(dst, src).then_inc(ld_const, 16)
            sp.wait_ge(setup_dve, 1)
            sp.dma_start(wr[0:CH, 0:E], router_w).then_inc(ld_const, 16)
            sp.dma_start(wr[CH:P, E:2 * E], router_w).then_inc(ld_const, 16)
            sp.wait_ge(ld_const, LOADS)
            for part in range(3):
                for b in range(2):
                    row = part * 2 * QN_ + b * QN_ + QB
                    col = bias_c + b * CH
                    sp.dma_start(cf[row:row + E, col:col + CH], expert_b).then_inc(ld_bias, 16)

            def load_a(r, pairs, step):
                if due(count := a_at(r, NGRP, step - 1, 0)):
                    sp.wait_ge(centred, count)
                src = xv[bass.ds(pairs[0], 1), :, step * TOK:(step + 1) * TOK].rearrange("a p t -> p (a t)")
                sp.dma_start(xa[:, step % 2, :], src).then_inc(ld_xa[step % 2], 16)

            def load_c(pairs, step):
                sl = step % 2
                pair = pairs[2] if step < STEPS else pairs[1]
                cols = slice((step % STEPS) * TOK, (step % STEPS + 1) * TOK)
                for b in range(2):
                    src = xv[bass.ds(pair, 1), b * CH:(b + 1) * CH, cols].rearrange("a p t -> p (a t)")
                    for half in range(2):
                        sp.dma_start(xd[half * CH:(half + 1) * CH, sl, b, :], src).then_inc(ld_xd[sl][b], 16)
                src = xv[bass.ds(pair, 1), :, cols].rearrange("a p t -> p (a t)")
                sp.dma_start(xc[:, sl, :], src).then_inc(ld_xc[sl], 16)

            def store(pairs, step):
                pair = pairs[2] if step >= 0 else pairs[3]
                n = step % STEPS
                dst = ov[bass.ds(pair, 1), :, n * TOK:(n + 1) * TOK].rearrange("a p t -> p (a t)")
                sp.dma_start(dst, ot[:, step % 2, :]).then_inc(stored[step % 2], 16)

            def body(r, A, Bp, C):
                pairs = [r - n if isinstance(r, int) else sp.snap(r - n) for n in range(4)]
                if A:
                    load_a(r, pairs, 0)
                for step in range(STEPS):
                    if A and step < STEPS - 1:
                        load_a(r, pairs, step + 1)
                    stores = C and not (first_pair(r) and step == 0)
                    if stores:
                        if due(count := c_at(r, 2, step - 1, 2)):
                            sp.wait_ge(final, count)
                    if follows(step, 1, Bp, C):
                        load_c(pairs, step + 1)
                    if stores:
                        store(pairs, step - 1)

            loop, rest = run_rounds(body)
            with sp.Fori(*loop) as r:
                body(r, True, True, True)
            for args in rest:
                body(*args)
            if due(count := c_at(PAIRS + 1, 2, STEPS - 1, 2)):
                sp.wait_ge(final, count)
            store([None, None, PAIRS - 1], STEPS - 1)
            for sl in range(2):
                sp.wait_ge(stored[sl], 16 * PAIRS * STEPS // 2)

        @block.tensor
        def _(pe):
            pe.wait_ge(ld_const, LOADS)
            pe.matmul(gb[:, 0, 0:KT * CH], centre, wst[:, :], start=True, stop=True)
            pe.matmul(gb[:, 1, 0:2 * E], centre, wr[:, :], start=True, stop=True)
            pe.matmul(gb[:, 2, 0:2], centre, mean_cols, start=True, stop=True).then_inc(setup_pe, 1)
            pe.wait_ge(setup_dve, 2)
            pe.wait_ge(setup_pool, 2)

            def centre_rows(r, step, g, C):
                if g == 0:
                    if due(count := slot_at(r, 0, step, 16)):
                        pe.wait_ge(ld_xa[step % 2], count)
                if due(count := a_at(r, NGRP, step, g if C else g - 1)):
                    pe.wait_ge(centred_out, count)
                bank = centre_bank(g, C)
                for j in range(GRP):
                    row = g * GRP + j
                    last = pe.matmul(bank[0:W, j * T1N:(j + 1) * T1N], xa[:, step % 2, row * W:(row + 1) * W],
                                     rhs1[:, :], start=True, stop=True)
                last.then_inc(centred, 1)

            def turn(r, step, Bp, C):
                if due(count := c_at(r, 1, step, 1)):
                    pe.wait_ge(part3, count)
                if due(count := c_at(r, 2, step - 1, 2)):
                    pe.wait_ge(a1_out, count)
                if Bp and (step == 3 or not C):
                    if due(count := b_at(r, B_ACT, 2)):
                        pe.wait_ge(b_act, count)
                for j in range(ROWS):
                    last = pe.transpose(misc16[0:SR, j * W:(j + 1) * W],
                                        parts[:, step % 2, j, :, :].rearrange("w a c -> w (a c)"), ident)
                last.then_inc(turned, 1)

            def spread_unit(r, step, u):
                if u >= UNITS:
                    step, u = step + 1, u - UNITS
                if u == 0:
                    if due(count := c_at(r, 1, step, 1)):
                        pe.wait_ge(s_ready, count)
                if due(count := c_at(r, UNITS, step, u - 1)):
                    pe.wait_ge(scaled, count)
                for c in range(2):
                    last = pe.matmul(gb[:, 2 * (u % 2) + c, 0:HALF], cg[0:SR, u * P:(u + 1) * P],
                                     s[:, step % 2, c * HALF:(c + 1) * HALF], start=True, stop=True)
                last.then_inc(spread, 1)

            def spread_a1(r, step, c):
                if c == 0:
                    if due(count := c_at(r, 1, step, 1)):
                        pe.wait_ge(s_ready, count)
                else:
                    if due(count := c_at(r, 2, step, c)):
                        pe.wait_ge(a1_out, count)
                pe.matmul(misc[:, 0:HALF], cg[0:SR, UNITS * P:(UNITS + 1) * P],
                          s[:, step % 2, c * HALF:(c + 1) * HALF], start=True, stop=True).then_inc(a1_spread, 1)

            def biases(r, step):
                for c in range(2):
                    if due(count := c_at(r, 2, step - 1, c + 1)):
                        pe.wait_ge(final, count)
                    for n, w in enumerate((bh, bl)):
                        pe.matmul(moe[:, c, 0:HALF], w[:, :], s[:, step % 2, c * HALF:(c + 1) * HALF],
                                  start=(n == 0), stop=False, skip_group_check=True)

            def experts(r, step, k, c):
                if c == 0:
                    if due(count := c_at(r, UNITS, step, 2 * k + 2)):
                        pe.wait_ge(scaled, count)
                for b in range(2):
                    last = pe.matmul(moe[b * CH:(b + 1) * CH, c, 0:HALF], wc[:, k * CH:(k + 1) * CH],
                                     gx[:, 2 * k + b, c * HALF:(c + 1) * HALF],
                                     start=False, stop=(k == KT - 1), skip_group_check=True)
                last.then_inc(mixed, 1)

            def convolve(r, C):
                if due(count := b_at(r, B_DVE, 3)):
                    pe.wait_ge(b_dve, count)
                if C:
                    if due(count := c_at(r, 2, 2, 2)):
                        pe.wait_ge(a1_out, count)
                for n in range(6):
                    ch, kh = n // 3, n % 3
                    last = pe.matmul(misc[0:W, 0:2 * H].rearrange("w (b h) -> w b h", b=2), band[:, n, :],
                                     pooled[:, ch, :, kh:kh + H], start=(n == 0), stop=(n == 5))
                last.then_inc(convolved, 1)

            def body(r, A, Bp, C):
                if first_pair(r):
                    spread_unit(r, 0, 2)
                    spread_unit(r, 0, 3)
                for step in range(STEPS):
                    ahead = follows(step, 1, Bp, C)
                    if ahead:
                        turn(r, step + 1, Bp, C)
                    for k in range(KT):
                        if A and k == 0:
                            centre_rows(r, step, 0, C)
                        if C:
                            if k == 0:
                                biases(r, step)
                            experts(r, step, k, 0)
                        if A and k > 0:
                            centre_rows(r, step, k, C)
                        if C:
                            if k < KT - 2 or ahead:
                                spread_unit(r, step, 2 * k + 4)
                            experts(r, step, k, 1)
                        if ahead and k in (1, 2):
                            spread_a1(r, step + 1, k - 1)
                        if Bp and step == 1 and k == KT - 1:
                            convolve(r, C)
                        if C and (k < KT - 2 or ahead):
                            spread_unit(r, step, 2 * k + 5)
                if Bp and not C:
                    spread_unit(r, STEPS, 0)
                    spread_unit(r, STEPS, 1)

            loop, rest = run_rounds(body)
            with pe.Fori(*loop) as r:
                body(r, True, True, True)
            for args in rest:
                body(*args)

        @block.vector
        def _(dve):
            dve.memset(wr[:, :], 0.0).then_inc(setup_dve, 1)
            dve.memset(eps[:, 0:1], EPS1)
            dve.memset(eps[:, 1:2], EPS2)
            dve.wait_ge(ld_const, LOADS)
            done = [0]

            def link(ins):
                done[0] += 1
                ins.then_inc(setup_step, 1)
                dve.wait_ge(setup_step, done[0])

            for n in range(6):
                link(dve.tensor_scalar(band[:, n, :], shift[0], cwb[:, 3 * n:3 * n + 1], None, ALU.mult))
                for kw in (1, 2):
                    link(dve.scalar_tensor_tensor(out=band[:, n, :], in0=shift[kw],
                                                  scalar=cwb[:, 3 * n + kw:3 * n + kw + 1], in1=band[:, n, :],
                                                  op0=ALU.mult, op1=ALU.add))
            link(dve.tensor_copy(cg[:, :], cg_load))
            link(dve.tensor_copy(rhs1[:, 0:P], centre))
            link(dve.tensor_copy(rhs1[:, P + 2 * E:T1N - 2], mean_cols))
            dve.wait_ge(setup_pe, 1)
            link(dve.tensor_copy(wc[:, :], gb[:, 0, 0:KT * CH]))
            link(dve.tensor_copy(rhs1[:, P:P + 2 * E], gb[:, 1, 0:2 * E]))
            link(dve.tensor_copy(rhs1[:, T1N - 2:T1N], gb[:, 2, 0:2]))
            dve.wait_ge(ld_bias, 6 * 16)
            link(dve.tensor_copy(bh[:, :], bias_base))
            link(dve.tensor_tensor(bl[:, :], bias_base, bh[:, :], ALU.subtract))
            dve.tensor_scalar(ncb[:, :], ncb[:, :], -1.0, None, ALU.mult).then_inc(setup_dve, 1)

            def channel_max(r, step):
                if due(count := a_at(r, NGRP, step, NGRP)):
                    dve.wait_ge(centred_out, count)
                to, cols = stats_at(step)
                dve.tensor_reduce(to[:, 0, cols], xsq[:, step % 2, 0, :, :], AX.X, ALU.max).then_inc(maxed, 1)

            def channel_sums(r, step):
                if due(count := a_at(r, 1, step, 1)):
                    dve.wait_ge(squared, count)
                to, cols = stats_at(step)
                dve.tensor_reduce(to[:, 1, cols], xsq[:, step % 2, 1, :, :], AX.X, ALU.add).then_inc(summed, LEVELS)

            def scale_unit(r, step, u):
                sl, b = step % 2, u % 2
                if u < 2:
                    if due(count := slot_at(r, 2, step, 32)):
                        dve.wait_ge(ld_xd[sl][b], count)
                if due(count := c_at(r, UNITS, step, u + 1)):
                    dve.wait_ge(spread, count)
                if due(count := c_at(r, 2 * KT, step - 1, 2 * (u // 2) + 2)):
                    dve.wait_ge(mixed, count)
                dve.tensor_tensor(gx[:, u, :].rearrange("p (c t) -> p c t", c=2),
                                  gb[:, 2 * (u % 2):2 * (u % 2) + 2, 0:HALF],
                                  xd[:, sl, b, :].rearrange("p (c t) -> p c t", c=2), ALU.mult).then_inc(scaled, 1)

            def finish(r, step, c):
                sl = step % 2
                if c == 0:
                    if due(count := c_at(r, 1, step, 1)):
                        dve.wait_ge(scaled_x, count)
                    if due(count := slot_at(r, 2, step - 2, 16)):
                        dve.wait_ge(stored[sl], count)
                if due(count := c_at(r, 2 * KT, step, 2 * KT - 1 + c)):
                    dve.wait_ge(mixed, count)
                cols = slice(c * HALF, (c + 1) * HALF)
                dve.tensor_tensor(ot[:, sl, cols], moe[:, c, 0:HALF], tt[:, sl, cols], ALU.add).then_inc(final, 1)

            def gate(r, step, place):
                def own(n):
                    if due(count := b_at(r, B_DVE, n)):
                        dve.wait_ge(b_dve, count)

                if (step, place) == (1, 3):
                    if due(count := b_at(r, B_ACT, 1)):
                        dve.wait_ge(b_act, count)
                    dve.reciprocal(r1[:, :], std[:, :]).then_inc(b_dve, 1)
                elif (step, place) == (1, 5):
                    if due(count := b_at(r, 1, 0)):
                        dve.wait_ge(convolved, count)
                    own(1)
                    dve.tensor_tensor(pooled[:, 0, :, 1:H + 1], stats[:, 0, :].rearrange(by_image, b=2),
                                      r1[:, :].rearrange(by_image, b=2), ALU.mult).then_inc(b_dve, 1)
                    dve.tensor_tensor(pooled[:, 1, :, 1:H + 1],
                                      logit_mean[:, :, 2 * E + 2:LN].rearrange("w h b -> w b h"),
                                      r1[:, :].rearrange(by_image, b=2), ALU.mult).then_inc(b_dve, 1)
                elif (step, place) == (2, 5):
                    if due(count := b_at(r, B_ACT, 2)):
                        dve.wait_ge(b_act, count)
                    dve.tensor_scalar(sg[:, :], ex[:, :], 1.0, None, ALU.add).then_inc(b_dve, 1)
                    own(4)
                    dve.reciprocal(v2[:, :], sg[:, :]).then_inc(b_dve, 1)
                elif (step, place) == (2, 7):
                    own(5)
                    dve.tensor_tensor(av[:, :], v2[:, :], r1[:, :], ALU.mult).then_inc(b_dve, 1)
                    own(6)
                    dve.tensor_scalar(ap1[:, :], av[:, :], 1.0, None, ALU.add).then_inc(b_dve, 1)
                    dve.tensor_tensor(am[:, :].rearrange("w (h b) -> w h b", b=2),
                                      av[:, :].rearrange("w (h b) -> w h b", b=2),
                                      logit_mean[:, :, 2 * E:2 * E + 2], ALU.mult).then_inc(b_dve, 1)
                    own(7)
                    dve.tensor_tensor(sg[:, :], ap1[:, :], ap1[:, :], ALU.mult).then_inc(b_dve, 1)
                    own(9)
                    dve.tensor_tensor(v2[:, :], sg[:, :], stats[:, 1, :], ALU.mult).then_inc(b_dve, 1)
                elif (step, place) == (3, 7):
                    if due(count := b_at(r, B_ACT, 3)):
                        dve.wait_ge(b_act, count)
                    dve.reciprocal(sg[:, :], std[:, :]).then_inc(b_dve, 1)
                    own(11)
                    dve.tensor_tensor(rho[:, :], sg[:, :], ap1[:, :], ALU.mult).then_inc(b_dve, 1)
                elif (step, place) == (5, 5):
                    if due(count := b_at(r, B_POOL, 2)):
                        dve.wait_ge(b_pool, count)
                    dve.tensor_reduce(top1[:, :], lg[:, :, :], AX.X, ALU.max).then_inc(b_dve, 1)
                elif (step, place) == (6, 5):
                    if due(count := b_at(r, B_POOL, 3)):
                        dve.wait_ge(b_pool, count)
                    dve.scalar_tensor_tensor(out=key[:, :, :], in0=dl[:, :, :], scalar=0.0, in1=prios,
                                             op0=ALU.is_ge, op1=ALU.mult).then_inc(b_dve, 1)
                elif (step, place) == (6, 7):
                    own(14)
                    dve.tensor_reduce(key_max[:, :], key[:, :, :], AX.X, ALU.max).then_inc(b_dve, 1)
                elif (step, place) == (7, 5):
                    own(15)
                    dve.tensor_tensor(oh1[:, :, :], prios, wide(key_max), ALU.is_equal).then_inc(b_dve, 1)
                elif (step, place) == (8, 5):
                    if due(count := b_at(r, B_POOL, 5)):
                        dve.wait_ge(b_pool, count)
                    dve.tensor_reduce(top2[:, :], lg[:, :, :], AX.X, ALU.max).then_inc(b_dve, 1)
                elif (step, place) == (8, 7):
                    own(17)
                    dve.tensor_tensor(ge[:, :, :], lg[:, :, :], wide(top2), ALU.is_ge).then_inc(b_dve, 1)
                elif (step, place) == (9, 5):
                    if due(count := b_at(r, B_POOL, 6)):
                        dve.wait_ge(b_pool, count)
                    dve.tensor_reduce(key_max[:, :], key[:, :, :], AX.X, ALU.max).then_inc(b_dve, 1)
                elif (step, place) == (9, 7):
                    if due(count := b_at(r, B_ACT, 4)):
                        dve.wait_ge(b_act, count)
                    dve.tensor_scalar(sg[:, :], ex[:, :], 1.0, None, ALU.add).then_inc(b_dve, 1)
                    own(20)
                    dve.reciprocal(g1[:, :], sg[:, :]).then_inc(b_dve, 1)
                    own(21)
                    dve.tensor_tensor(g2[:, :], ex[:, :], g1[:, :], ALU.mult).then_inc(b_dve, 1)
                elif (step, place) == (10, 5):
                    own(19)
                    dve.tensor_tensor(oh2[:, :, :], prios, wide(key_max), ALU.is_equal).then_inc(b_dve, 1)
                elif (step, place) == (11, 7):
                    if due(count := c_at(r, 1, STEPS, 0)):
                        dve.wait_ge(rest1, count)
                    dve.tensor_scalar(q_tokens[:, :, QA], ap1[:, :], 1.0, None, ALU.mult).then_inc(b_dve, 1)
                    dve.tensor_scalar(q_tokens[:, :, QM], am[:, :], 1.0, None, ALU.mult).then_inc(b_dve, 1)

            def reduce_channels(r, step, A, Bp, C):
                if (Bp and step == 0) or (A and step > 0):
                    if step == 1:
                        if due(count := at(r, 0, JOINS, 0)):
                            dve.wait_ge(joined, count)
                    channel_max(r, step - 1)
                    if not C:
                        channel_sums(r, step - 1)

            def body(r, A, Bp, C):
                for step in range(STEPS):
                    for u in range(UNITS):
                        if C:
                            scale_unit(r, step, u)
                            if u < 2 and not (first_pair(r) and step == 0):
                                finish(r, step - 1, u)
                        if u == 3:
                            reduce_channels(r, step, A, Bp, C)
                        if Bp:
                            gate(r, step, u)

            loop, rest = run_rounds(body)
            with dve.Fori(*loop) as r:
                body(r, True, True, True)
            for args in rest:
                body(*args)
            for c in range(2):
                finish(PAIRS + 1, STEPS - 1, c)

        @block.scalar
        def _(act):
            act.wait_ge(setup_dve, 2)

            def centred_to_sbuf(r, step, g, C):
                sl = step % 2
                if g == 0:
                    if due(count := a_at(r, LEVELS, step - 1, 0)):
                        act.wait_ge(summed, count)
                    if due(count := a_at(r, 1, step - 1, 0)):
                        act.wait_ge(maxed, count)
                if due(count := a_at(r, NGRP, step, g + 1)):
                    act.wait_ge(centred, count)
                src = centre_bank(g, C)[0:W, 0:GRP * T1N].rearrange("w (j n) -> w j n", j=GRP)
                act.activation(xsq[:, sl, 0, 2 * GRP * g:2 * GRP * (g + 1), :]
                               .rearrange("w (j b) c -> w j (b c)", b=2), src[:, :, 0:P], ACT.Copy)
                if step >= EARLY and g == 0:
                    if due(count := b_at(r, B_POOL, 1)):
                        act.wait_ge(b_pool, count)
                to, row = logits_at(step)
                row += g * GRP
                act.activation(to[:, row:row + GRP, :], src[:, :, P:T1N], ACT.Copy).then_inc(centred_out, 1)

            def square(r, step):
                if due(count := a_at(r, NGRP, step, NGRP)):
                    act.wait_ge(centred_out, count)
                act.activation(xsq[:, step % 2, 1, :, :], xsq[:, step % 2, 0, :, :], ACT.Square) \
                   .then_inc(squared, 1)

            def part_one(r, step):
                n = step % STEPS
                if due(count := c_at(r, 1, step - 2, 1)):
                    act.wait_ge(turned, count)
                if step >= STEPS:
                    if due(count := b_at(r, B_POOL, B_POOL)):
                        act.wait_ge(b_pool, count)
                    if due(count := b_at(r, B_DVE, B_DVE)):
                        act.wait_ge(b_dve, count)
                act.activation(parts[:, step % 2, :, 0, :], q[:, n * ROWS:(n + 1) * ROWS, :], ACT.Copy) \
                   .then_inc(part1, 1)

            def part_two(r, step):
                if due(count := c_at(r, 1, step, 1)):
                    act.wait_ge(rest1, count)
                act.activation(parts[:, step % 2, :, 1, :], res[:, step % 2, :, :], ACT.Copy).then_inc(part2, 1)

            def turned_to_sbuf(r, step):
                if due(count := c_at(r, 1, step, 1)):
                    act.wait_ge(turned, count)
                if due(count := c_at(r, 2 * KT, step - 2, 2 * KT)):
                    act.wait_ge(mixed, count)
                act.activation(s[:, step % 2, :], misc16[0:SR, 0:TOK], ACT.Copy).then_inc(s_ready, 1)

            def a1_to_sbuf(r, step, c):
                if due(count := c_at(r, 2, step, c + 1)):
                    act.wait_ge(a1_spread, count)
                if c == 0:
                    if due(count := c_at(r, 1, step - 2, 1)):
                        act.wait_ge(scaled_x, count)
                act.activation(a1s[:, step % 2, c * HALF:(c + 1) * HALF], misc[:, 0:HALF], ACT.Copy).then_inc(a1_out, 1)

            def join_early(r):
                if due(count := b_at(r, B_DVE, 12)):
                    act.wait_ge(b_dve, count)
                if due(count := a_at(r, 1, EARLY, 0)):
                    act.wait_ge(maxed, count)
                if due(count := a_at(r, LEVELS, EARLY, 0)):
                    act.wait_ge(summed, count)
                if due(count := a_at(r, NGRP, EARLY, 0)):
                    act.wait_ge(centred_out, count)
                act.activation(stats[:, :, 0:EARLY * ROWS * 2], early_s[:, :, :], ACT.Copy).then_inc(joined, 1)
                act.activation(logit_mean[:, 0:EARLY * ROWS, :], early_l[:, :, :], ACT.Copy).then_inc(joined, 1)

            def gate(r, step):
                if step == 0:
                    if due(count := a_at(r, LEVELS, 0, 0)):
                        act.wait_ge(summed, count)
                    if due(count := at(r, 0, JOINS, 0)):
                        act.wait_ge(joined, count)
                    act.activation(std[:, :], stats[:, 1, :], ACT.Sqrt, bias=eps[:, 0:1], scale=1.0 / CH) \
                       .then_inc(b_act, 1)
                elif step == 1:
                    if due(count := b_at(r, 1, 1)):
                        act.wait_ge(convolved, count)
                    act.activation(ex[:, :].rearrange(by_image, b=2),
                                   misc[0:W, 0:2 * H].rearrange("w (b h) -> w b h", b=2),
                                   ACT.Exp, bias=ncb[:, :], scale=-1.0).then_inc(b_act, 1)
                elif step == 3:
                    if due(count := b_at(r, B_DVE, 10)):
                        act.wait_ge(b_dve, count)
                    act.activation(std[:, :], v2[:, :], ACT.Sqrt, bias=eps[:, 1:2], scale=1.0 / CH) \
                       .then_inc(b_act, 1)
                elif step == 9:
                    if due(count := b_at(r, B_DVE, 17)):
                        act.wait_ge(b_dve, count)
                    act.activation(ex[:, :], top2[:, :], ACT.Exp).then_inc(b_act, 1)

            def body(r, A, Bp, C):
                for step in range(STEPS):
                    if follows(step, 1, Bp, C):
                        turned_to_sbuf(r, step + 1)
                    if A and step == 0:
                        if due(count := at(r, 0, JOINS, 0)):
                            act.wait_ge(joined, count)
                    if A:
                        centred_to_sbuf(r, step, 0, C)
                    if follows(step, 2, Bp, C):
                        part_one(r, step + 2)
                    if Bp and step in (3, 9):
                        gate(r, step)
                    for g in range(1, NGRP):
                        if A:
                            centred_to_sbuf(r, step, g, C)
                        if g < 3 and follows(step, 1, Bp, C):
                            a1_to_sbuf(r, step + 1, g - 1)
                        if g == 1 and follows(step, 2, Bp, C):
                            part_two(r, step + 2)
                    if Bp and step in (0, 1):
                        gate(r, step)
                    if A:
                        square(r, step)
                        if step == 11:
                            join_early(r)

            loop, rest = run_rounds(body)
            with act.Fori(*loop) as r:
                body(r, True, True, True)
            for args in rest:
                body(*args)

        @block.gpsimd
        def _(pool):
            pool.memset(low[:, :], -BIG).then_inc(setup_pool, 1)
            pool.memset(pooled[:, :, :, :], 0.0).then_inc(setup_pool, 1)
            pool.wait_ge(setup_pool, 2)

            def channel_sums(r, step):
                if due(count := a_at(r, 1, step, 1)):
                    pool.wait_ge(squared, count)
                src = xsq[:, step % 2, 1, :, :]
                to, cols = stats_at(step)
                lo, n = 0, CH // 2
                for level in range(LEVELS):
                    if due(count := a_at(r, LEVELS, step, level)):
                        pool.wait_ge(summed, count)
                    if n > 1:
                        dst = tree[:, lo:lo + 2 * ROWS * n].rearrange("w (g c) -> w g c", c=n)
                        lo += 2 * ROWS * n
                    else:
                        dst = to[:, 1, cols].unsqueeze(2)
                    pool.tensor_tensor(dst, src[:, :, 0:n], src[:, :, n:2 * n], ALU.add).then_inc(summed, 1)
                    src = dst
                    n //= 2

            def rest_one(r, step):
                n = step % STEPS
                if due(count := c_at(r, 1, step, 1)):
                    pool.wait_ge(part1, count)
                if due(count := c_at(r, 1, step - 2, 1)):
                    pool.wait_ge(part3, count)
                pool.tensor_tensor(res[:, step % 2, :, :], q[:, n * ROWS:(n + 1) * ROWS, :],
                                   parts[:, step % 2, :, 0, :], ALU.subtract).then_inc(rest1, 1)

            def part_three(r, step):
                if due(count := c_at(r, 1, step, 1)):
                    pool.wait_ge(part2, count)
                pool.tensor_tensor(parts[:, step % 2, :, 2, :], res[:, step % 2, :, :],
                                   parts[:, step % 2, :, 1, :], ALU.subtract).then_inc(part3, 1)

            def scale_x(r, step):
                sl = step % 2
                if due(count := slot_at(r, 2, step, 16)):
                    pool.wait_ge(ld_xc[sl], count)
                if due(count := c_at(r, 2, step, 2)):
                    pool.wait_ge(a1_out, count)
                if due(count := c_at(r, 2, step - 2, 2)):
                    pool.wait_ge(final, count)
                pool.tensor_tensor(tt[:, sl, :], xc[:, sl, :], a1s[:, sl, :], ALU.mult).then_inc(scaled_x, 1)

            def gate(r, step, late):
                def own(n):
                    if due(count := b_at(r, B_POOL, n)):
                        pool.wait_ge(b_pool, count)

                if (step, late) == (4, True):
                    if due(count := b_at(r, B_DVE, 12)):
                        pool.wait_ge(b_dve, count)
                    own(0)
                    pool.tensor_tensor(lg[:, :, :].rearrange("w (h b) e -> w h b e", b=2),
                                       logit_mean[:, :, 0:2 * E].rearrange("w h (b e) -> w h b e", b=2),
                                       rho[:, :].rearrange("w (h b) -> w h b", b=2).unsqueeze(3)
                                       .to_broadcast([W, H, 2, E]), ALU.mult).then_inc(b_pool, 1)
                    own(1)
                    pool.tensor_tensor(lg[:, :, :], lg[:, :, :],
                                       brb[:, :].unsqueeze(1).to_broadcast([W, 2 * H, E]), ALU.add) \
                        .then_inc(b_pool, 1)
                elif (step, late) == (5, True):
                    if due(count := b_at(r, B_DVE, 13)):
                        pool.wait_ge(b_dve, count)
                    pool.tensor_tensor(dl[:, :, :], lg[:, :, :], wide(top1), ALU.subtract).then_inc(b_pool, 1)
                elif (step, late) == (7, True):
                    if due(count := b_at(r, B_DVE, 16)):
                        pool.wait_ge(b_dve, count)
                    own(3)
                    pool.tensor_tensor(lg[:, :, :], oh1[:, :, :],
                                       low[:, :].unsqueeze(2).to_broadcast([W, 2 * H, E]), ALU.mult) \
                        .then_inc(b_pool, 1)
                    own(4)
                    pool.tensor_tensor(lg[:, :, :], lg[:, :, :], dl[:, :, :], ALU.add).then_inc(b_pool, 1)
                elif (step, late) == (9, False):
                    if due(count := b_at(r, B_DVE, 18)):
                        pool.wait_ge(b_dve, count)
                    pool.tensor_tensor(key[:, :, :], ge[:, :, :], prios, ALU.mult).then_inc(b_pool, 1)
                elif (step, late) == (10, False):
                    if due(count := b_at(r, B_DVE, 22)):
                        pool.wait_ge(b_dve, count)
                    pool.tensor_tensor(lg[:, :, :], oh1[:, :, :], wide(g1), ALU.mult).then_inc(b_pool, 1)
                elif (step, late) == (10, True):
                    if due(count := b_at(r, B_DVE, 23)):
                        pool.wait_ge(b_dve, count)
                    pool.tensor_tensor(dl[:, :, :], oh2[:, :, :], wide(g2), ALU.mult).then_inc(b_pool, 1)
                elif (step, late) == (11, False):
                    own(8)
                    if due(count := c_at(r, 1, STEPS, 0)):
                        pool.wait_ge(rest1, count)
                    pool.tensor_tensor(q_tokens[:, :, QB:QB + E], lg[:, :, :], dl[:, :, :], ALU.add) \
                        .then_inc(b_pool, 1)
                elif (step, late) == (11, True):
                    own(9)
                    pool.tensor_tensor(q_tokens[:, :, QG:QG + E], q_tokens[:, :, QB:QB + E], wide(rho), ALU.mult) \
                        .then_inc(b_pool, 1)

            def body(r, A, Bp, C):
                for step in range(STEPS):
                    if follows(step, 2, Bp, C):
                        rest_one(r, step + 2)
                    if Bp:
                        gate(r, step, False)
                    if C and ((Bp and step == 0) or (A and step > 0)):
                        if step == 1:
                            if due(count := at(r, 0, JOINS, 0)):
                                pool.wait_ge(joined, count)
                        channel_sums(r, step - 1)
                    if follows(step, 2, Bp, C):
                        part_three(r, step + 2)
                    if follows(step, 1, Bp, C):
                        scale_x(r, step + 1)
                    if Bp:
                        gate(r, step, True)

            loop, rest = run_rounds(body)
            with pool.Fori(*loop) as r:
                body(r, True, True, True)
            for args in rest:
                body(*args)


_INS = ['x', 'L0_conv_conv_w', 'L0_conv_conv_b', 'L0_ffn_router_w', 'L0_ffn_router_b', 'L0_ffn_expert_w',
        'L0_ffn_expert_b']
_OUT = ((B, CH, H, W), 'float32')


def kernel(**inputs):
    import concourse.bacc as _bacc
    from concourse.bass_utils import run_bass_kernel_spmd as _run

    nc = _bacc.Bacc("TRN2", target_bir_lowering=False, num_devices=1)
    arrays, args = {}, []
    named = [(name, np.ascontiguousarray(inputs[name])) for name in _INS]
    named += list(zip(("const_f", "const_g"), constant_arrays()))
    for name, a in named:
        arrays[f"in_{name}_dram"] = a
        args.append(nc.dram_tensor(f"in_{name}_dram", a.shape, mybir.dt.from_np(a.dtype), kind="ExternalInput").ap())
    args.append(nc.dram_tensor("out_0_dram", _OUT[0], mybir.dt.from_np(np.dtype(_OUT[1])), kind="ExternalOutput").ap())
    gated_expert_program(nc, *args)
    r = _run(nc, [arrays], core_ids=[0])
    return r.results[0]["out_0_dram"]
```

```python
from contextlib import ExitStack

import numpy as np

import concourse.bass as bass
from concourse import mybir

F32 = mybir.dt.float32
BF16 = mybir.dt.bfloat16
F16 = mybir.dt.float16
ALU = mybir.AluOpType
ACT = mybir.ActivationFunctionType
AX = mybir.AxisListType

B, CH, H, W = 16, 64, 112, 112
E = 8
P = 128
PAIRS = B // 2
ROWS = 8
STEPS = H // ROWS
TOK = ROWS * W
HALF = TOK // 2
GRP = 2
NGRP = ROWS // GRP
KT = E // 2
UNITS = 2 * KT
LN = 2 * E + 4
T1N = P + LN
XA = 7
EARLY = 6
QN = 2 * E + 2
SR = 3 * 2 * QN
QG, QB, QA, QM = 0, E, 2 * E, 2 * E + 1
EPS1, EPS2 = 1e-6, 1e-5
BIG = 1e30


def constant_arrays():
    f = np.zeros((P, 2 * P + 2 + 3 * W + E), np.float32)
    for b in range(2):
        lo = b * CH
        f[lo:lo + CH, lo:lo + CH] = np.eye(CH) - 1.0 / CH
        f[lo:lo + CH, P + b] = 1.0 / CH
    o = P + 2
    for kw in range(3):
        for w_out in range(W):
            w_in = w_out + kw - 1
            if 0 <= w_in < W:
                f[w_in, o + kw * W + w_out] = 1.0
    o += 3 * W
    f[:, o:o + E] = np.arange(E, 0, -1)
    o += E
    for part in range(3):
        for b in range(2):
            f[part * 2 * QN + b * QN + QM, o + b * CH:o + (b + 1) * CH] = -1.0
    g = np.zeros((P, (UNITS + 1) * P + P), np.float32)
    for part in range(3):
        for b in range(2):
            row = part * 2 * QN + b * QN
            for k in range(KT):
                for e in range(2):
                    lo = (2 * k + b) * P + e * CH
                    g[row + QG + 2 * k + e, lo:lo + CH] = 1.0
            g[row + QA, UNITS * P + b * CH:UNITS * P + (b + 1) * CH] = 1.0
    g[:, (UNITS + 1) * P:] = np.eye(P)
    return f, g


def gated_expert_program(nc, x, conv_w, conv_b, router_w, router_b, expert_w, expert_b, const_f, const_g, out):
    xv = x.rearrange("(q b) c h w -> q (b c) (h w)", b=2)
    ov = out.rearrange("(q b) c h w -> q (b c) (h w)", b=2)

    with ExitStack() as ctx:
        def sb(name, shape, dt=F32):
            return ctx.enter_context(nc.sbuf_tensor(name, shape, dt))

        def ps(name, shape, dt=F32):
            return ctx.enter_context(nc.psum_tensor(name, shape, dt))

        def sem(name):
            return ctx.enter_context(nc.semaphore(name))

        cf = sb("cf", [P, 2 * P + 2 + 3 * W + E])
        cg = sb("cg", [P, (UNITS + 2) * P], BF16)
        gx = sb("gx", [P, UNITS, TOK])
        gx_flat = gx[:, :, :].rearrange("p a t -> p (a t)")
        centre = cf[:, 0:P]
        mean_cols = cf[:, P:P + 2]
        shift = [cf[0:W, P + 2 + kw * W:P + 2 + (kw + 1) * W] for kw in range(3)]
        prio_c = P + 2 + 3 * W
        prio_in = cf[0:W, prio_c:prio_c + E]
        bias_c = prio_c + E
        bias_base = cf[0:SR, bias_c:bias_c + P]
        cg_load = gx_flat[:, 0:(UNITS + 2) * P]
        wst = gx_flat[:, (UNITS + 2) * P:(UNITS + 2) * P + KT * CH]
        ident = cg[0:W, (UNITS + 1) * P:(UNITS + 1) * P + W]
        rhs1 = sb("rhs1", [P, T1N])
        wr = sb("wr", [P, 2 * E])
        wc = sb("wc", [P, KT * CH])
        bh = sb("bh", [SR, P], F16)
        bl = sb("bl", [SR, P], F16)
        cwb = sb("cwb", [W, 18])
        ncb = sb("ncb", [W, 1])
        prio = sb("prio", [W, E], BF16)
        brb = sb("brb", [W, E])
        band = sb("band", [W, 6, W])
        eps = sb("eps", [W, 2])
        xa = sb("xa", [P, XA, TOK])
        xsq = sb("xsq", [W, 2, 2, 2 * ROWS, CH])
        tree = sb("tree", [W, 2 * ROWS * (CH - 2)])
        early_l = sb("early_l", [W, EARLY * ROWS, LN])
        early_s = sb("early_s", [W, 2, EARLY * ROWS * 2])
        logit_mean = sb("logit_mean", [W, H, LN])
        stats = sb("stats", [W, 2, 2 * H])
        pooled = sb("pooled", [W, 2, 2, H + 2])
        std = sb("std", [W, 2 * H])
        r1 = sb("r1", [W, 2 * H])
        ex = sb("ex", [W, 2 * H])
        sg = sb("sg", [W, 2 * H])
        av = sb("av", [W, 2 * H])
        ap1 = sb("ap1", [W, 2 * H])
        am = sb("am", [W, 2 * H])
        v2 = sb("v2", [W, 2 * H])
        rho = sb("rho", [W, 2 * H])
        top = sb("top", [W, 2 * H])
        key_max = sb("key_max", [W, 2 * H], BF16)
        g1 = sb("g1", [W, 2 * H])
        g2 = sb("g2", [W, 2 * H])
        lg = sb("lg", [W, 2 * H, E])
        band_part = lg[:, :, :].rearrange("w n e -> w (n e)")[:, 0:W]
        dl = sb("dl", [W, 2 * H, E])
        key = sb("key", [W, 2 * H, E], BF16)
        half_key = sb("half_key", [W, 2 * H, 4], BF16)
        quarter_key = sb("quarter_key", [W, 2 * H, 2], BF16)
        oh1 = sb("oh1", [W, 2 * H, E], BF16)
        ge = sb("ge", [W, 2 * H, E], BF16)
        oh2 = sb("oh2", [W, 2 * H, E], BF16)
        q = sb("q", [W, H, 2 * QN])
        res = sb("res", [W, 2, ROWS, 2 * QN])
        parts = sb("parts", [W, 2, ROWS, 3, 2 * QN], BF16)
        s = sb("s", [SR, 2, TOK], BF16)
        xd = sb("xd", [P, 2, 2, TOK])
        xc = sb("xc", [P, 2, TOK])
        a1s = sb("a1s", [P, 2, TOK])
        tt = sb("tt", [P, 2, TOK])
        ot = sb("ot", [P, 2, TOK])

        gb = ps("gb", [P, 4, 512])
        moe = ps("moe", [P, 2, 512])
        t1 = ps("t1", [P, 512])
        misc = ps("misc", [P, 512])
        misc16 = misc[:, :].bitcast(BF16)

        ld_first = sem("ld_first")
        ld_const = sem("ld_const")
        ld_bias = sem("ld_bias")
        setup_pe = sem("setup_pe")
        setup_dve = sem("setup_dve")
        setup_pool = sem("setup_pool")
        ld_xa = [sem(f"ld_xa{i}") for i in range(XA)]
        ld_xd = [[sem(f"ld_xd{i}{b}") for b in range(2)] for i in range(2)]
        ld_xc = [sem(f"ld_xc{i}") for i in range(2)]
        stored = [sem(f"stored{i}") for i in range(2)]
        centred = sem("centred")
        centred_out = sem("centred_out")
        squared = sem("squared")
        maxed = sem("maxed")
        summed = sem("summed")
        joined = sem("joined")
        b_act = sem("b_act")
        b_dve = sem("b_dve")
        b_pool = sem("b_pool")
        convolved = sem("convolved")
        part1 = sem("part1")
        rest1 = sem("rest1")
        part2 = sem("part2")
        part3 = sem("part3")
        turned = sem("turned")
        s_ready = sem("s_ready")
        spread = sem("spread")
        scaled = sem("scaled")
        a1_spread = sem("a1_spread")
        a1_out = sem("a1_out")
        scaled_x = sem("scaled_x")
        mixed = sem("mixed")
        final = sem("final")

        FIRST_LOADS, LOADS, BIAS_LOADS = 3 * 16, 5 * 16, 6 * 16
        POOL_SETUP = 1 + 1 + 6 * 5 + 1 + 1 + 2

        def at(r, first, per, n):
            return (r - first) * per + n if isinstance(r, int) else r * per + (n - first * per)

        def due(count):
            return not isinstance(count, int) or count > 0

        def a_at(r, per_step, step, n):
            return at(r, 0, per_step * STEPS, per_step * step + n)

        def b_at(r, per_round, n):
            return at(r, 1, per_round, n)

        def c_at(r, per_step, step, n):
            return at(r, 2, per_step * STEPS, per_step * step + n)

        def slot_at(r, first, step, add):
            return at(r, first, add * STEPS // 2, add * (step // 2 + 1))

        B_DVE, B_POOL, B_ACT, JOINS, LEVELS = 30, 8, 6, 2, 6

        def first_pair(r):
            return isinstance(r, int) and r == 2

        def follows(step, n, Bp, C):
            return C if step + n < STEPS else Bp

        def splits(step, Bp, C):
            if Bp and not C:
                return (STEPS, STEPS + 1) if step == STEPS - 2 else ()
            return (step + 2,) if follows(step, 2, Bp, C) else ()

        def centre_banks(r, C):
            if C:
                return [t1]
            return [t1, moe[:, 0, :], moe[:, 1, :]] + ([misc] if r == 0 else [])

        def centre_bank(r, step, g, C):
            banks = centre_banks(r, C)
            return banks[(NGRP * step + g) % len(banks)]

        def logits_at(step):
            return (early_l, step * ROWS) if step < EARLY else (logit_mean, step * ROWS)

        def stats_at(step):
            n = step % STEPS
            return (early_s if n < EARLY else stats), slice(2 * ROWS * n, 2 * ROWS * (n + 1))

        q_tokens = q[:, :, :].rearrange("w h (b k) -> w (h b) k", b=2)
        by_image = "w (h b) -> w b h"

        def wide(v):
            return v[:, :].unsqueeze(2).to_broadcast([W, 2 * H, E])

        prios = prio[:, :].unsqueeze(1).to_broadcast([W, 2 * H, E])

        def router(eng, r, step, late):
            def own(n):
                if due(count := b_at(r, B_POOL, n)):
                    eng.wait_ge(b_pool, count)

            if (step, late) == (3, True):
                if due(count := b_at(r, B_DVE, 12)):
                    eng.wait_ge(b_dve, count)
                own(0)
                eng.tensor_tensor(lg[:, :, :].rearrange("w (h b) e -> w h b e", b=2),
                                  logit_mean[:, :, 0:2 * E].rearrange("w h (b e) -> w h b e", b=2),
                                  rho[:, :].rearrange("w (h b) -> w h b", b=2).unsqueeze(3)
                                  .to_broadcast([W, H, 2, E]), ALU.mult).then_inc(b_pool, 1)
                own(1)
                eng.tensor_tensor(lg[:, :, :], lg[:, :, :],
                                  brb[:, :].unsqueeze(1).to_broadcast([W, 2 * H, E]), ALU.add) \
                    .then_inc(b_pool, 1)
            elif (step, late) == (4, True):
                if due(count := b_at(r, B_DVE, 13)):
                    eng.wait_ge(b_dve, count)
                eng.tensor_tensor(dl[:, :, :], lg[:, :, :], wide(top), ALU.subtract).then_inc(b_pool, 1)
            elif (step, late) == (8, True):
                if due(count := b_at(r, B_DVE, 21)):
                    eng.wait_ge(b_dve, count)
                eng.tensor_tensor(key[:, :, :], ge[:, :, :], prios, ALU.mult).then_inc(b_pool, 1)
            elif (step, late) == (10, False):
                if due(count := b_at(r, B_DVE, 24)):
                    eng.wait_ge(b_dve, count)
                eng.tensor_tensor(lg[:, :, :], oh1[:, :, :], wide(g1), ALU.mult).then_inc(b_pool, 1)
            elif (step, late) == (10, True):
                if due(count := b_at(r, B_DVE, 28)):
                    eng.wait_ge(b_dve, count)
                eng.tensor_tensor(dl[:, :, :], oh2[:, :, :], wide(g2), ALU.mult).then_inc(b_pool, 1)
            elif (step, late) == (11, False):
                own(6)
                if due(count := c_at(r, 1, STEPS, 0)):
                    eng.wait_ge(rest1, count)
                eng.tensor_tensor(q_tokens[:, :, QB:QB + E], lg[:, :, :], dl[:, :, :], ALU.add) \
                    .then_inc(b_pool, 1)
            elif (step, late) == (11, True):
                own(7)
                eng.tensor_tensor(q_tokens[:, :, QG:QG + E], q_tokens[:, :, QB:QB + E], wide(rho), ALU.mult) \
                    .then_inc(b_pool, 1)

        block = ctx.enter_context(nc.Block())

        @block.sync
        def _(sp):
            sp.dma_start(cf[:, :], const_f).then_inc(ld_first, 16)
            sp.wait_ge(setup_dve, 1)
            sp.dma_start(wr[0:CH, 0:E], router_w).then_inc(ld_first, 16)
            sp.dma_start(wr[CH:P, E:2 * E], router_w).then_inc(ld_first, 16)

            def load_a(pair, step):
                src = xv[bass.ds(pair, 1), :, step * TOK:(step + 1) * TOK].rearrange("a p t -> p (a t)")
                sp.dma_start(xa[:, step % XA, :], src).then_inc(ld_xa[step % XA], 16)

            def load_c(pairs, step):
                sl = step % 2
                pair = pairs[2] if step < STEPS else pairs[1]
                cols = slice((step % STEPS) * TOK, (step % STEPS + 1) * TOK)
                for b in range(2):
                    src = xv[bass.ds(pair, 1), b * CH:(b + 1) * CH, cols].rearrange("a p t -> p (a t)")
                    for half in range(2):
                        sp.dma_start(xd[half * CH:(half + 1) * CH, sl, b, :], src).then_inc(ld_xd[sl][b], 16)
                src = xv[bass.ds(pair, 1), :, cols].rearrange("a p t -> p (a t)")
                sp.dma_start(xc[:, sl, :], src).then_inc(ld_xc[sl], 16)

            def store(pairs, step):
                pair = pairs[2] if step >= 0 else pairs[3]
                n = step % STEPS
                dst = ov[bass.ds(pair, 1), :, n * TOK:(n + 1) * TOK].rearrange("a p t -> p (a t)")
                sp.dma_start(dst, ot[:, step % 2, :]).then_inc(stored[step % 2], 16)

            def loads_a(r, pair, steps):
                for step in steps:
                    if due(count := a_at(r, NGRP, step - XA + 1, 0)):
                        sp.wait_ge(centred, count)
                    load_a(pair, step)

            def body(r, A, Bp, C):
                pairs = [r - n if isinstance(r, int) else sp.snap(r - n) for n in range(4)]
                lead = 2 if C else XA - 1
                for step in range(STEPS):
                    if A:
                        first = (2 if isinstance(r, int) and r == 0 else 0) if step == 0 else step + lead
                        loads_a(r, pairs[0], range(first, min(step + lead + 1, STEPS)))
                    stores = C and not (first_pair(r) and step == 0)
                    if stores:
                        if due(count := c_at(r, 2, step - 1, 2)):
                            sp.wait_ge(final, count)
                    if follows(step, 1, Bp, C):
                        load_c(pairs, step + 1)
                    if stores:
                        store(pairs, step - 1)

            load_a(0, 0)
            load_a(0, 1)
            for dst, src in (
                (cg_load, const_g),
                (wst.rearrange("p (k c) -> p k c", k=KT), expert_w.rearrange("(k e) d c -> (e d) k c", e=2)),
                (cwb[:, :], conv_w.rearrange("o c h w -> o (c h w)").to_broadcast([W, 18])),
                (ncb[:, :], conv_b.rearrange("(o n) -> o n", o=1).to_broadcast([W, 1])),
                (brb[:, :], router_b.rearrange("(o n) -> o n", o=1).to_broadcast([W, E])),
            ):
                sp.dma_start(dst, src).then_inc(ld_const, 16)
            sp.wait_ge(ld_first, FIRST_LOADS)
            for part in range(3):
                for b in range(2):
                    row = part * 2 * QN + b * QN + QB
                    col = bias_c + b * CH
                    sp.dma_start(cf[row:row + E, col:col + CH], expert_b).then_inc(ld_bias, 16)

            body(0, True, False, False)
            body(1, True, True, False)
            body(2, True, True, True)
            with sp.Fori(3, PAIRS) as r:
                body(r, True, True, True)
            body(PAIRS, False, True, True)
            body(PAIRS + 1, False, False, True)
            if due(count := c_at(PAIRS + 1, 2, STEPS - 1, 2)):
                sp.wait_ge(final, count)
            store([None, None, PAIRS - 1], STEPS - 1)
            for sl in range(2):
                sp.wait_ge(stored[sl], 16 * PAIRS * STEPS // 2)

        @block.tensor
        def _(pe):
            pe.wait_ge(ld_first, FIRST_LOADS)
            pe.matmul(gb[:, 1, 0:2 * E], centre, wr[:, :], start=True, stop=True)
            pe.matmul(gb[:, 2, 0:2], centre, mean_cols, start=True, stop=True).then_inc(setup_pe, 1)
            pe.wait_ge(setup_dve, 2)

            def centre_rows(r, step, g, C):
                if g == 0:
                    if due(count := at(r, 0, STEPS // XA * 16, (step // XA + 1) * 16)):
                        pe.wait_ge(ld_xa[step % XA], count)
                if due(count := a_at(r, NGRP, step, g + 1 - len(centre_banks(r, C)))):
                    pe.wait_ge(centred_out, count)
                bank = centre_bank(r, step, g, C)
                for j in range(GRP):
                    row = g * GRP + j
                    last = pe.matmul(bank[0:W, j * T1N:(j + 1) * T1N], xa[:, step % XA, row * W:(row + 1) * W],
                                     rhs1[:, :], start=True, stop=True)
                last.then_inc(centred, 1)

            def turn(r, step, Bp, C):
                if due(count := c_at(r, 1, step, 1)):
                    pe.wait_ge(part3, count)
                if due(count := c_at(r, 2, step - 1, 2)):
                    pe.wait_ge(a1_out, count)
                if Bp and (step == 3 or not C):
                    if due(count := b_at(r, B_ACT, 2)):
                        pe.wait_ge(b_act, count)
                for j in range(ROWS):
                    last = pe.transpose(misc16[0:SR, j * W:(j + 1) * W],
                                        parts[:, step % 2, j, :, :].rearrange("w a c -> w (a c)"), ident)
                last.then_inc(turned, 1)

            def spread_unit(r, step, u):
                if u >= UNITS:
                    step, u = step + 1, u - UNITS
                if u == 0:
                    if due(count := c_at(r, 1, step, 1)):
                        pe.wait_ge(s_ready, count)
                if due(count := c_at(r, UNITS, step, u - 1)):
                    pe.wait_ge(scaled, count)
                for c in range(2):
                    last = pe.matmul(gb[:, 2 * (u % 2) + c, 0:HALF], cg[0:SR, u * P:(u + 1) * P],
                                     s[:, step % 2, c * HALF:(c + 1) * HALF], start=True, stop=True)
                last.then_inc(spread, 1)

            def spread_a1(r, step, c):
                if c == 0:
                    if due(count := c_at(r, 1, step, 1)):
                        pe.wait_ge(s_ready, count)
                else:
                    if due(count := c_at(r, 2, step, c)):
                        pe.wait_ge(a1_out, count)
                pe.matmul(misc[:, 0:HALF], cg[0:SR, UNITS * P:(UNITS + 1) * P],
                          s[:, step % 2, c * HALF:(c + 1) * HALF], start=True, stop=True).then_inc(a1_spread, 1)

            def biases(r, step, c):
                if due(count := c_at(r, 2, step - 1, c + 1)):
                    pe.wait_ge(final, count)
                for n, w in enumerate((bh, bl)):
                    pe.matmul(moe[:, c, 0:HALF], w[:, :], s[:, step % 2, c * HALF:(c + 1) * HALF],
                              start=(n == 0), stop=False, skip_group_check=True)

            def experts(r, step, k, c):
                if c == 0:
                    if due(count := c_at(r, UNITS, step, 2 * k + 2)):
                        pe.wait_ge(scaled, count)
                for b in range(2):
                    last = pe.matmul(moe[b * CH:(b + 1) * CH, c, 0:HALF], wc[:, k * CH:(k + 1) * CH],
                                     gx[:, 2 * k + b, c * HALF:(c + 1) * HALF],
                                     start=False, stop=(k == KT - 1), skip_group_check=True)
                last.then_inc(mixed, 1)

            def convolve(r, C):
                if due(count := b_at(r, B_DVE, 3)):
                    pe.wait_ge(b_dve, count)
                if C:
                    if due(count := c_at(r, 2, 2, 2)):
                        pe.wait_ge(a1_out, count)
                for n in range(6):
                    ch, kh = n // 3, n % 3
                    last = pe.matmul(misc[0:W, 0:2 * H].rearrange("w (b h) -> w b h", b=2), band[:, n, :],
                                     pooled[:, ch, :, kh:kh + H], start=(n == 0), stop=(n == 5))
                last.then_inc(convolved, 1)

            def body(r, A, Bp, C):
                if first_pair(r):
                    spread_unit(r, 0, 2)
                    spread_unit(r, 0, 3)
                for step in range(STEPS):
                    ahead = follows(step, 1, Bp, C)
                    if ahead:
                        turn(r, step + 1, Bp, C)
                    for k in range(KT):
                        if A and k == 0:
                            centre_rows(r, step, 0, C)
                        if C:
                            if k == 0:
                                biases(r, step, 0)
                            experts(r, step, k, 0)
                        if Bp and not C and step == STEPS - 1 and k < 2:
                            spread_unit(r, STEPS, k)
                        if A and k > 0 and not C:
                            centre_rows(r, step, k, C)
                        if C:
                            if k < KT - 2 or ahead:
                                spread_unit(r, step, 2 * k + 4)
                            if k == 0:
                                biases(r, step, 1)
                            experts(r, step, k, 1)
                        if ahead and k in (1, 2):
                            spread_a1(r, step + 1, k - 1)
                        if Bp and step == 1 and k == KT - 1:
                            convolve(r, C)
                        if C and (k < KT - 2 or ahead):
                            spread_unit(r, step, 2 * k + 5)
                        if A and C and k < KT - 1:
                            centre_rows(r, step, k + 1, C)

            body(0, True, False, False)
            pe.wait_ge(ld_const, LOADS)
            pe.matmul(gb[:, 0, 0:KT * CH], centre, wst, start=True, stop=True).then_inc(setup_pe, 1)
            pe.wait_ge(setup_pool, POOL_SETUP)
            pe.wait_ge(setup_dve, 3)
            body(1, True, True, False)
            body(2, True, True, True)
            with pe.Fori(3, PAIRS) as r:
                body(r, True, True, True)
            body(PAIRS, False, True, True)
            body(PAIRS + 1, False, False, True)

        @block.vector
        def _(dve):
            dve.memset(wr[:, :], 0.0).then_inc(setup_dve, 1)
            dve.memset(eps[:, 0:1], EPS1)
            dve.memset(eps[:, 1:2], EPS2)
            dve.wait_ge(ld_first, FIRST_LOADS)
            dve.tensor_copy(rhs1[:, 0:P], centre)
            dve.tensor_copy(rhs1[:, P + 2 * E:T1N - 2], mean_cols)
            dve.wait_ge(setup_pe, 1)
            dve.tensor_copy(rhs1[:, P:P + 2 * E], gb[:, 1, 0:2 * E])
            dve.tensor_copy(rhs1[:, T1N - 2:T1N], gb[:, 2, 0:2]).then_inc(setup_dve, 1)

            def channel_max(r, step):
                if due(count := a_at(r, NGRP, step, NGRP)):
                    dve.wait_ge(centred_out, count)
                to, cols = stats_at(step)
                dve.tensor_reduce(to[:, 0, cols], xsq[:, step % 2, 0, :, :], AX.X, ALU.max).then_inc(maxed, 1)

            def channel_sums(r, step):
                if due(count := a_at(r, 1, step, 1)):
                    dve.wait_ge(squared, count)
                to, cols = stats_at(step)
                dve.tensor_reduce(to[:, 1, cols], xsq[:, step % 2, 1, :, :], AX.X, ALU.add).then_inc(summed, LEVELS)

            def scale_unit(r, step, u):
                sl, b = step % 2, u % 2
                if u < 2:
                    if due(count := slot_at(r, 2, step, 32)):
                        dve.wait_ge(ld_xd[sl][b], count)
                if due(count := c_at(r, UNITS, step, u + 1)):
                    dve.wait_ge(spread, count)
                if due(count := c_at(r, 2 * KT, step - 1, 2 * (u // 2) + 2)):
                    dve.wait_ge(mixed, count)
                dve.tensor_tensor(gx[:, u, :].rearrange("p (c t) -> p c t", c=2),
                                  gb[:, 2 * (u % 2):2 * (u % 2) + 2, 0:HALF],
                                  xd[:, sl, b, :].rearrange("p (c t) -> p c t", c=2), ALU.mult).then_inc(scaled, 1)

            def finish(r, step, c):
                sl = step % 2
                if c == 0:
                    if due(count := c_at(r, 1, step, 1)):
                        dve.wait_ge(scaled_x, count)
                    if due(count := slot_at(r, 2, step - 2, 16)):
                        dve.wait_ge(stored[sl], count)
                if due(count := c_at(r, 2 * KT, step, 2 * KT - 1 + c)):
                    dve.wait_ge(mixed, count)
                cols = slice(c * HALF, (c + 1) * HALF)
                dve.tensor_tensor(ot[:, sl, cols], moe[:, c, 0:HALF], tt[:, sl, cols], ALU.add).then_inc(final, 1)

            def halve_keys(own, n):
                own(n)
                dve.tensor_tensor(half_key[:, :, :], key[:, :, 0:4], key[:, :, 4:8], ALU.max).then_inc(b_dve, 1)

            def largest_key(own, n):
                own(n + 1)
                dve.tensor_tensor(quarter_key[:, :, :], half_key[:, :, 0:2], half_key[:, :, 2:4], ALU.max) \
                   .then_inc(b_dve, 1)
                own(n + 2)
                dve.tensor_tensor(key_max[:, :], quarter_key[:, :, 0], quarter_key[:, :, 1], ALU.max) \
                   .then_inc(b_dve, 1)

            def gate(r, step, place):
                def own(n):
                    if due(count := b_at(r, B_DVE, n)):
                        dve.wait_ge(b_dve, count)

                first, second = slice(0, H), slice(H, 2 * H)
                if (step, place) == (1, 2):
                    if due(count := b_at(r, B_ACT, 1)):
                        dve.wait_ge(b_act, count)
                    dve.reciprocal(r1[:, first], std[:, first])
                elif (step, place) == (1, 4):
                    dve.reciprocal(r1[:, second], std[:, second]).then_inc(b_dve, 1)
                elif (step, place) == (1, 5):
                    if due(count := b_at(r, 1, 0)):
                        dve.wait_ge(convolved, count)
                    own(1)
                    dve.tensor_tensor(pooled[:, 0, :, 1:H + 1], stats[:, 0, :].rearrange(by_image, b=2),
                                      r1[:, :].rearrange(by_image, b=2), ALU.mult).then_inc(b_dve, 1)
                    dve.tensor_tensor(pooled[:, 1, :, 1:H + 1],
                                      logit_mean[:, :, 2 * E + 2:LN].rearrange("w h b -> w b h"),
                                      r1[:, :].rearrange(by_image, b=2), ALU.mult).then_inc(b_dve, 1)
                elif (step, place) == (2, 4):
                    if due(count := b_at(r, B_ACT, 2)):
                        dve.wait_ge(b_act, count)
                    dve.tensor_scalar(sg[:, :], ex[:, :], 1.0, None, ALU.add).then_inc(b_dve, 1)
                    own(4)
                    dve.reciprocal(v2[:, first], sg[:, first])
                elif (step, place) == (2, 6):
                    dve.reciprocal(v2[:, second], sg[:, second]).then_inc(b_dve, 1)
                    own(5)
                    dve.tensor_tensor(av[:, :], v2[:, :], r1[:, :], ALU.mult).then_inc(b_dve, 1)
                elif (step, place) == (2, 7):
                    own(6)
                    dve.tensor_scalar(ap1[:, :], av[:, :], 1.0, None, ALU.add).then_inc(b_dve, 1)
                    dve.tensor_tensor(am[:, :].rearrange("w (h b) -> w h b", b=2),
                                      av[:, :].rearrange("w (h b) -> w h b", b=2),
                                      logit_mean[:, :, 2 * E:2 * E + 2], ALU.mult).then_inc(b_dve, 1)
                elif (step, place) == (3, 0):
                    own(8)
                    dve.tensor_tensor(sg[:, :], ap1[:, :], ap1[:, :], ALU.mult).then_inc(b_dve, 1)
                    own(9)
                    dve.tensor_tensor(v2[:, :], sg[:, :], stats[:, 1, :], ALU.mult).then_inc(b_dve, 1)
                elif (step, place) == (3, 5):
                    if due(count := b_at(r, B_ACT, 3)):
                        dve.wait_ge(b_act, count)
                    dve.reciprocal(sg[:, first], std[:, first])
                elif (step, place) == (3, 7):
                    dve.reciprocal(sg[:, second], std[:, second]).then_inc(b_dve, 1)
                    own(11)
                    dve.tensor_tensor(rho[:, :], sg[:, :], ap1[:, :], ALU.mult).then_inc(b_dve, 1)
                elif (step, place) in ((4, 6), (4, 7)):
                    if place == 6:
                        if due(count := b_at(r, B_POOL, 2)):
                            dve.wait_ge(b_pool, count)
                    rows = first if place == 6 else second
                    ins = dve.tensor_reduce(top[:, rows], lg[:, rows, :], AX.X, ALU.max)
                    if place == 7:
                        ins.then_inc(b_dve, 1)
                elif (step, place) in ((5, 4), (5, 6)):
                    if place == 4:
                        if due(count := b_at(r, B_POOL, 3)):
                            dve.wait_ge(b_pool, count)
                    rows = first if place == 4 else second
                    ins = dve.scalar_tensor_tensor(out=key[:, rows, :], in0=dl[:, rows, :], scalar=0.0,
                                                   in1=prios[:, rows, :], op0=ALU.is_ge, op1=ALU.mult)
                    if place == 6:
                        ins.then_inc(b_dve, 1)
                elif (step, place) == (5, 7):
                    halve_keys(own, 14)
                elif (step, place) == (6, 0):
                    largest_key(own, 14)
                elif (step, place) == (6, 4):
                    if due(count := b_at(r, B_ACT, 4)):
                        dve.wait_ge(b_act, count)
                    dve.tensor_tensor(oh1[:, :, :], prios, ge[:, :, :], ALU.is_equal).then_inc(b_dve, 1)
                elif (step, place) in ((6, 6), (7, 0)):
                    if place == 6:
                        own(18)
                    rows = first if place == 6 else second
                    ins = dve.scalar_tensor_tensor(out=lg[:, rows, :], in0=oh1[:, rows, :], scalar=-BIG,
                                                   in1=dl[:, rows, :], op0=ALU.mult, op1=ALU.add)
                    if place == 0:
                        ins.then_inc(b_dve, 1)
                elif (step, place) in ((7, 5), (7, 7)):
                    if place == 5:
                        own(19)
                    rows = first if place == 5 else second
                    ins = dve.tensor_reduce(top[:, rows], lg[:, rows, :], AX.X, ALU.max)
                    if place == 7:
                        ins.then_inc(b_dve, 1)
                elif (step, place) in ((8, 4), (8, 6)):
                    if place == 4:
                        own(20)
                    rows = first if place == 4 else second
                    ins = dve.tensor_tensor(ge[:, rows, :], lg[:, rows, :], wide(top)[:, rows, :], ALU.is_ge)
                    if place == 6:
                        ins.then_inc(b_dve, 1)
                elif (step, place) == (9, 4):
                    if due(count := b_at(r, B_ACT, 5)):
                        dve.wait_ge(b_act, count)
                    dve.tensor_scalar(sg[:, :], ex[:, :], 1.0, None, ALU.add).then_inc(b_dve, 1)
                    own(22)
                    dve.reciprocal(g1[:, first], sg[:, first])
                elif (step, place) == (9, 6):
                    dve.reciprocal(g1[:, second], sg[:, second]).then_inc(b_dve, 1)
                    own(23)
                    dve.tensor_tensor(g2[:, :], ex[:, :], g1[:, :], ALU.mult).then_inc(b_dve, 1)
                elif (step, place) == (9, 7):
                    if due(count := b_at(r, B_POOL, 4)):
                        dve.wait_ge(b_pool, count)
                    halve_keys(own, 24)
                elif (step, place) == (10, 1):
                    largest_key(own, 24)
                elif (step, place) == (10, 6):
                    if due(count := b_at(r, B_ACT, 6)):
                        dve.wait_ge(b_act, count)
                    dve.tensor_tensor(oh2[:, :, :], prios, ge[:, :, :], ALU.is_equal).then_inc(b_dve, 1)
                elif (step, place) == (11, 7):
                    if due(count := c_at(r, 1, STEPS, 0)):
                        dve.wait_ge(rest1, count)
                    dve.tensor_scalar(q_tokens[:, :, QA], ap1[:, :], 1.0, None, ALU.mult).then_inc(b_dve, 1)
                    dve.tensor_scalar(q_tokens[:, :, QM], am[:, :], 1.0, None, ALU.mult).then_inc(b_dve, 1)

            def reduce_channels(r, step, A, Bp, C):
                if (Bp and step == 0) or (A and step > 0):
                    if step == 1:
                        if due(count := at(r, 0, JOINS, 0)):
                            dve.wait_ge(joined, count)
                    channel_max(r, step - 1)
                    if not C and (step == 0 or not Bp):
                        channel_sums(r, step - 1)

            def body(r, A, Bp, C):
                for step in range(STEPS):
                    if Bp and not C:
                        router(dve, r, step, False)
                    for u in range(UNITS):
                        if C:
                            scale_unit(r, step, u)
                            if u in (1, 2) and not (first_pair(r) and step == 0):
                                finish(r, step - 1, u - 1)
                        if u == 3:
                            reduce_channels(r, step, A, Bp, C)
                        if Bp:
                            gate(r, step, u)
                    if Bp and not C:
                        router(dve, r, step, True)

            body(0, True, False, False)
            dve.wait_ge(setup_pe, 2)
            dve.tensor_copy(wc[:, :], gb[:, 0, 0:KT * CH]).then_inc(setup_dve, 1)
            dve.wait_ge(setup_pool, POOL_SETUP)
            body(1, True, True, False)
            body(2, True, True, True)
            with dve.Fori(3, PAIRS) as r:
                body(r, True, True, True)
            body(PAIRS, False, True, True)
            body(PAIRS + 1, False, False, True)
            for c in range(2):
                finish(PAIRS + 1, STEPS - 1, c)

        @block.scalar
        def _(act):
            act.wait_ge(setup_dve, 2)

            def centred_to_sbuf(r, step, g, C):
                sl = step % 2
                if g == 0:
                    if due(count := a_at(r, LEVELS, step - 1, 0)):
                        act.wait_ge(summed, count)
                    if due(count := a_at(r, 1, step - 1, 0)):
                        act.wait_ge(maxed, count)
                if due(count := a_at(r, NGRP, step, g + 1)):
                    act.wait_ge(centred, count)
                src = centre_bank(r, step, g, C)[0:W, 0:GRP * T1N].rearrange("w (j n) -> w j n", j=GRP)
                act.activation(xsq[:, sl, 0, 2 * GRP * g:2 * GRP * (g + 1), :]
                               .rearrange("w (j b) c -> w j (b c)", b=2), src[:, :, 0:P], ACT.Copy)
                if step >= EARLY and g == 0:
                    if due(count := b_at(r, B_POOL, 1)):
                        act.wait_ge(b_pool, count)
                to, row = logits_at(step)
                row += g * GRP
                act.activation(to[:, row:row + GRP, :], src[:, :, P:T1N], ACT.Copy).then_inc(centred_out, 1)

            def square(r, step):
                if due(count := a_at(r, NGRP, step, NGRP)):
                    act.wait_ge(centred_out, count)
                act.activation(xsq[:, step % 2, 1, :, :], xsq[:, step % 2, 0, :, :], ACT.Square) \
                   .then_inc(squared, 1)

            def part_one(r, step):
                n = step % STEPS
                if due(count := c_at(r, 1, step - 2, 1)):
                    act.wait_ge(turned, count)
                if step >= STEPS:
                    if due(count := b_at(r, B_POOL, B_POOL)):
                        act.wait_ge(b_pool, count)
                    if due(count := b_at(r, B_DVE, B_DVE)):
                        act.wait_ge(b_dve, count)
                act.activation(parts[:, step % 2, :, 0, :], q[:, n * ROWS:(n + 1) * ROWS, :], ACT.Copy) \
                   .then_inc(part1, 1)

            def part_two(r, step):
                if due(count := c_at(r, 1, step, 1)):
                    act.wait_ge(rest1, count)
                act.activation(parts[:, step % 2, :, 1, :], res[:, step % 2, :, :], ACT.Copy).then_inc(part2, 1)

            def turned_to_sbuf(r, step):
                if due(count := c_at(r, 1, step, 1)):
                    act.wait_ge(turned, count)
                if due(count := c_at(r, 2 * KT, step - 2, 2 * KT)):
                    act.wait_ge(mixed, count)
                act.activation(s[:, step % 2, :], misc16[0:SR, 0:TOK], ACT.Copy).then_inc(s_ready, 1)

            def a1_to_sbuf(r, step, c):
                if due(count := c_at(r, 2, step, c + 1)):
                    act.wait_ge(a1_spread, count)
                if c == 0:
                    if due(count := c_at(r, 1, step - 2, 1)):
                        act.wait_ge(scaled_x, count)
                act.activation(a1s[:, step % 2, c * HALF:(c + 1) * HALF], misc[:, 0:HALF], ACT.Copy) \
                   .then_inc(a1_out, 1)

            def join_early(r):
                if due(count := b_at(r, B_DVE, 12)):
                    act.wait_ge(b_dve, count)
                if due(count := a_at(r, 1, EARLY, 0)):
                    act.wait_ge(maxed, count)
                if due(count := a_at(r, LEVELS, EARLY, 0)):
                    act.wait_ge(summed, count)
                if due(count := a_at(r, NGRP, EARLY, 0)):
                    act.wait_ge(centred_out, count)
                act.activation(stats[:, :, 0:EARLY * ROWS * 2], early_s[:, :, :], ACT.Copy).then_inc(joined, 1)
                act.activation(logit_mean[:, 0:EARLY * ROWS, :], early_l[:, :, :], ACT.Copy).then_inc(joined, 1)

            def gate(r, step):
                if step == 0:
                    if due(count := a_at(r, LEVELS, 0, 0)):
                        act.wait_ge(summed, count)
                    if due(count := at(r, 0, JOINS, 0)):
                        act.wait_ge(joined, count)
                    act.activation(std[:, :], stats[:, 1, :], ACT.Sqrt, bias=eps[:, 0:1], scale=1.0 / CH) \
                       .then_inc(b_act, 1)
                elif step == 1:
                    if due(count := b_at(r, 1, 1)):
                        act.wait_ge(convolved, count)
                    act.activation(ex[:, :].rearrange(by_image, b=2),
                                   misc[0:W, 0:2 * H].rearrange("w (b h) -> w b h", b=2),
                                   ACT.Exp, bias=ncb[:, :], scale=-1.0).then_inc(b_act, 1)
                elif step == 3:
                    if due(count := b_at(r, B_DVE, 10)):
                        act.wait_ge(b_dve, count)
                    act.activation(std[:, :], v2[:, :], ACT.Sqrt, bias=eps[:, 1:2], scale=1.0 / CH) \
                       .then_inc(b_act, 1)
                elif step == 6:
                    if due(count := b_at(r, B_DVE, 17)):
                        act.wait_ge(b_dve, count)
                    act.activation(ge[:, :, :], wide(key_max), ACT.Copy).then_inc(b_act, 1)
                elif step == 8:
                    if due(count := b_at(r, B_DVE, 20)):
                        act.wait_ge(b_dve, count)
                    act.activation(ex[:, :], top[:, :], ACT.Exp).then_inc(b_act, 1)
                elif step == 10:
                    if due(count := b_at(r, B_DVE, 27)):
                        act.wait_ge(b_dve, count)
                    act.activation(ge[:, :, :], wide(key_max), ACT.Copy).then_inc(b_act, 1)

            def body(r, A, Bp, C):
                for step in range(STEPS):
                    if follows(step, 1, Bp, C):
                        turned_to_sbuf(r, step + 1)
                    if A and step == 0:
                        if due(count := at(r, 0, JOINS, 0)):
                            act.wait_ge(joined, count)
                    if A:
                        centred_to_sbuf(r, step, 0, C)
                    for n in splits(step, Bp, C):
                        part_one(r, n)
                    if Bp and step in (3, 6, 8, 10):
                        gate(r, step)
                    for g in range(1, NGRP):
                        if A:
                            centred_to_sbuf(r, step, g, C)
                        if g < 3 and follows(step, 1, Bp, C):
                            a1_to_sbuf(r, step + 1, g - 1)
                        if g == 1:
                            for n in splits(step, Bp, C):
                                part_two(r, n)
                        if Bp and (step, g) == (0, 2):
                            gate(r, step)
                    if Bp and step == 1:
                        gate(r, step)
                    if A:
                        square(r, step)
                        if step == 11:
                            join_early(r)

            body(0, True, False, False)
            act.wait_ge(setup_pool, POOL_SETUP)
            body(1, True, True, False)
            body(2, True, True, True)
            with act.Fori(3, PAIRS) as r:
                body(r, True, True, True)
            body(PAIRS, False, True, True)
            body(PAIRS + 1, False, False, True)

        @block.gpsimd
        def _(pool):
            done = [0]

            def link(ins):
                done[0] += 1
                ins.then_inc(setup_pool, 1)
                pool.wait_ge(setup_pool, done[0])

            link(pool.memset(pooled[:, :, :, :], 0.0))
            pool.wait_ge(ld_first, FIRST_LOADS)
            pool.wait_ge(ld_const, LOADS)
            link(pool.tensor_copy(prio[:, :], prio_in))
            for n in range(6):
                for kw in range(3):
                    weight = cwb[:, 3 * n + kw:3 * n + kw + 1].to_broadcast([W, W])
                    link(pool.tensor_tensor(band[:, n, :] if kw == 0 else band_part, shift[kw], weight, ALU.mult))
                    if kw > 0:
                        link(pool.tensor_tensor(band[:, n, :], band[:, n, :], band_part, ALU.add))
            link(pool.tensor_scalar(ncb[:, :], ncb[:, :], -1.0, None, ALU.mult))
            link(pool.tensor_copy(cg[:, :], cg_load))
            pool.wait_ge(ld_bias, BIAS_LOADS)
            link(pool.tensor_copy(bh[:, :], bias_base))
            link(pool.tensor_tensor(bl[:, :], bias_base, bh[:, :], ALU.subtract))

            def channel_sums(r, step):
                if due(count := a_at(r, 1, step, 1)):
                    pool.wait_ge(squared, count)
                src = xsq[:, step % 2, 1, :, :]
                to, cols = stats_at(step)
                lo, n = 0, CH // 2
                for level in range(LEVELS):
                    if due(count := a_at(r, LEVELS, step, level)):
                        pool.wait_ge(summed, count)
                    if n > 1:
                        dst = tree[:, lo:lo + 2 * ROWS * n].rearrange("w (g c) -> w g c", c=n)
                        lo += 2 * ROWS * n
                    else:
                        dst = to[:, 1, cols].unsqueeze(2)
                    pool.tensor_tensor(dst, src[:, :, 0:n], src[:, :, n:2 * n], ALU.add).then_inc(summed, 1)
                    src = dst
                    n //= 2

            def rest_one(r, step):
                n = step % STEPS
                if due(count := c_at(r, 1, step, 1)):
                    pool.wait_ge(part1, count)
                if due(count := c_at(r, 1, step - 2, 1)):
                    pool.wait_ge(part3, count)
                pool.tensor_tensor(res[:, step % 2, :, :], q[:, n * ROWS:(n + 1) * ROWS, :],
                                   parts[:, step % 2, :, 0, :], ALU.subtract).then_inc(rest1, 1)

            def part_three(r, step):
                if due(count := c_at(r, 1, step, 1)):
                    pool.wait_ge(part2, count)
                pool.tensor_tensor(parts[:, step % 2, :, 2, :], res[:, step % 2, :, :],
                                   parts[:, step % 2, :, 1, :], ALU.subtract).then_inc(part3, 1)

            def scale_x(r, step):
                sl = step % 2
                if due(count := slot_at(r, 2, step, 16)):
                    pool.wait_ge(ld_xc[sl], count)
                if due(count := c_at(r, 2, step, 2)):
                    pool.wait_ge(a1_out, count)
                if due(count := c_at(r, 2, step - 2, 2)):
                    pool.wait_ge(final, count)
                pool.tensor_tensor(tt[:, sl, :], xc[:, sl, :], a1s[:, sl, :], ALU.mult).then_inc(scaled_x, 1)

            def body(r, A, Bp, C):
                for step in range(STEPS):
                    for n in splits(step, Bp, C):
                        rest_one(r, n)
                    if not C:
                        for n in splits(step, Bp, C):
                            part_three(r, n)
                    if Bp and C:
                        router(pool, r, step, False)
                    if (Bp and C and step == 0) or (A and Bp and step > 0):
                        if step == 1:
                            if due(count := at(r, 0, JOINS, 0)):
                                pool.wait_ge(joined, count)
                        channel_sums(r, step - 1)
                    if C:
                        for n in splits(step, Bp, C):
                            part_three(r, n)
                    if follows(step, 1, Bp, C):
                        scale_x(r, step + 1)
                    if Bp and C:
                        router(pool, r, step, True)

            body(0, True, False, False)
            body(1, True, True, False)
            body(2, True, True, True)
            with pool.Fori(3, PAIRS) as r:
                body(r, True, True, True)
            body(PAIRS, False, True, True)
            body(PAIRS + 1, False, False, True)


_INS = ['x', 'L0_conv_conv_w', 'L0_conv_conv_b', 'L0_ffn_router_w', 'L0_ffn_router_b', 'L0_ffn_expert_w',
        'L0_ffn_expert_b']
_OUT = ((B, CH, H, W), 'float32')


def kernel(**inputs):
    import concourse.bacc as _bacc
    from concourse.bass_utils import run_bass_kernel_spmd as _run

    nc = _bacc.Bacc("TRN2", target_bir_lowering=False, num_devices=1)
    arrays, args = {}, []
    named = [(name, np.ascontiguousarray(inputs[name])) for name in _INS]
    named += list(zip(("const_f", "const_g"), constant_arrays()))
    for name, a in named:
        arrays[f"in_{name}_dram"] = a
        args.append(nc.dram_tensor(f"in_{name}_dram", a.shape, mybir.dt.from_np(a.dtype), kind="ExternalInput").ap())
    args.append(nc.dram_tensor("out_0_dram", _OUT[0], mybir.dt.from_np(np.dtype(_OUT[1])), kind="ExternalOutput").ap())
    gated_expert_program(nc, *args)
    r = _run(nc, [arrays], core_ids=[0])
    return r.results[0]["out_0_dram"]
```
